# Optimizing a Trainium2 kernel written in Bass

```python
import numpy as np
import jax
import jax.numpy as jnp

def _softmax(x, axis=-1):
    return jax.nn.softmax(x, axis=axis)
def _gelu(x):
    return jax.nn.gelu(x, approximate=True)
def _silu(x):
    return jax.nn.silu(x)
def _sigmoid(x):
    return jax.nn.sigmoid(x)
def _layernorm(x, axis=-1, eps=1e-5):
    m = jnp.mean(x, axis=axis, keepdims=True)
    v = jnp.var(x, axis=axis, keepdims=True)
    return (x - m) / jnp.sqrt(v + eps)
def _scatter_add(tgt, idx, src, axis=0):
    return tgt.at[idx].add(src)
def _segment_sum(src, seg, n):
    return jax.ops.segment_sum(src, seg, n)

kernel_name = 'mk_adj_resnorm_d2_adj_512_681569'

def setup_inputs(seed: int = 0):
    np.random.seed(seed)
    _w = jnp.asarray
    def _rec_inputs():
        import jax
        import jax.numpy as jnp
        _gk = jax.random.key(seed)
        x = -0.0002928 + 1 * jax.random.normal(jax.random.fold_in(_gk, 1), (4096, 512), jnp.float32)
        _a = jax.random.bernoulli(jax.random.fold_in(_gk, 2), 0.00195312, (4096, 4096))
        _a = jnp.logical_or(_a, jnp.swapaxes(_a, -1, -2))
        _a = jnp.logical_or(_a, jnp.eye(4096, dtype=bool))
        _af = _a.astype(jnp.float32)
        _af = _af * jax.random.uniform(jax.random.fold_in(_gk, 3), (4096, 4096), jnp.float32, 0.05, 5.41998)
        adj = _af
        return x, adj
    x, adj = _rec_inputs()
    def _L0_gnn_setup():
        import jax, jax.numpy as jnp
        import numpy as np
        N = 8192
        D = 512
        key = jax.random.key(seed)
        ks = jax.random.split(key, 6)
        s = 1.0 / np.sqrt(D)
        return {'x': jax.random.normal(ks[0], (N, D), jnp.float32), 'spatial_encoding': jax.random.normal(ks[1], (N, N), jnp.float32), 'edge_encoding': jax.random.normal(ks[2], (N, N), jnp.float32), 'Wq': jax.random.normal(ks[3], (D, D), jnp.float32) * s, 'bq': jnp.zeros((D,), jnp.float32), 'Wk': jax.random.normal(ks[4], (D, D), jnp.float32) * s, 'bk': jnp.zeros((D,), jnp.float32), 'Wv': jax.random.normal(ks[5], (D, D), jnp.float32) * s, 'bv': jnp.zeros((D,), jnp.float32)}
    _L0_gnn_all = _L0_gnn_setup()
    _L0_gnn_in = {k: v for k, v in _L0_gnn_all.items() if k in ('Wq', 'bq', 'Wk', 'bk', 'Wv', 'bv', )}
    del _L0_gnn_all

    def _L1_gnn_setup():
        import jax, jax.numpy as jnp
        import numpy as np
        NEG_INF = -10000000000.0
        LEAKY_ALPHA = 0.2
        key = jax.random.key(seed)
        k1, k2, k3, k4, k5 = jax.random.split(key, 5)
        N, F, H, D = (4096, 512, 8, 64)
        X = jax.random.normal(k1, (N, F), dtype=jnp.float32)
        A = jax.random.randint(k2, (N, N), 0, 2).astype(jnp.float32)
        W = jax.random.normal(k3, (H, F, D), dtype=jnp.float32) * (1.0 / np.sqrt(F))
        b = jnp.zeros((H, D), dtype=jnp.float32)
        a_self = jax.random.normal(k4, (H, D), dtype=jnp.float32) * (1.0 / np.sqrt(D))
        a_neigh = jax.random.normal(k5, (H, D), dtype=jnp.float32) * (1.0 / np.sqrt(D))
        return {'X': X, 'A': A, 'W': W, 'b': b, 'a_self': a_self, 'a_neigh': a_neigh}
    _L1_gnn_all = _L1_gnn_setup()
    _L1_gnn_in = {k: v for k, v in _L1_gnn_all.items() if k in ('W', 'b', 'a_self', 'a_neigh', )}
    del _L1_gnn_all

    return {
        "x": x,
        "adj": adj,
        "L0_gnn_Wq": _L0_gnn_in["Wq"],
        "L0_gnn_bq": _L0_gnn_in["bq"],
        "L0_gnn_Wk": _L0_gnn_in["Wk"],
        "L0_gnn_bk": _L0_gnn_in["bk"],
        "L0_gnn_Wv": _L0_gnn_in["Wv"],
        "L0_gnn_bv": _L0_gnn_in["bv"],
        "L1_gnn_W": _L1_gnn_in["W"],
        "L1_gnn_b": _L1_gnn_in["b"],
        "L1_gnn_a_self": _L1_gnn_in["a_self"],
        "L1_gnn_a_neigh": _L1_gnn_in["a_neigh"],
    }

def reference(x, adj, L0_gnn_Wq, L0_gnn_bq, L0_gnn_Wk, L0_gnn_bk, L0_gnn_Wv, L0_gnn_bv, L1_gnn_W, L1_gnn_b, L1_gnn_a_self, L1_gnn_a_neigh):
    import jax
    import jax.numpy as jnp
    def _L0_gnn_ref(x, spatial_encoding, edge_encoding, Wq, bq, Wk, bk, Wv, bv):
        import jax, jax.numpy as jnp
        import numpy as np
        N = 8192
        D = 512
        q = x @ Wq.T + bq
        k = x @ Wk.T + bk
        v = x @ Wv.T + bv
        scale = 1.0 / jnp.sqrt(jnp.asarray(q.shape[-1], q.dtype))
        a = q @ k.T * scale + spatial_encoding + edge_encoding
        attn = jax.nn.softmax(a, axis=-1)
        return attn @ v

    def _L1_gnn_ref(X, A, W, b, a_self, a_neigh):
        import jax, jax.numpy as jnp
        import numpy as np
        NEG_INF = -10000000000.0
        LEAKY_ALPHA = 0.2
        feats = jnp.einsum('nf,hfd->hnd', X, W)
        e_self = jnp.einsum('hnd,hd->hn', feats, a_self)
        e_neigh = jnp.einsum('hnd,hd->hn', feats, a_neigh)
        dense = e_self[:, :, None] + e_neigh[:, None, :]
        dense = jnp.where(dense >= 0, dense, LEAKY_ALPHA * dense)
        mask = NEG_INF * (1.0 - A)
        dense = dense + mask[None, :, :]
        attn = jax.nn.softmax(dense, axis=-1)
        out = jnp.einsum('hnm,hmd->hnd', attn, feats) + b[:, None, :]
        H, N, D = out.shape
        out = jnp.transpose(out, (1, 0, 2)).reshape(N, H * D)
        return jax.nn.relu(out)

    x = _layernorm(x + _L0_gnn_ref(x, adj, adj, L0_gnn_Wq, L0_gnn_bq, L0_gnn_Wk, L0_gnn_bk, L0_gnn_Wv, L0_gnn_bv), axis=-1)
    x = _layernorm(x + _L1_gnn_ref(x, adj, L1_gnn_W, L1_gnn_b, L1_gnn_a_self, L1_gnn_a_neigh), axis=-1)
    return x


_drawn_inputs = setup_inputs


def setup_inputs(seed=0):
    import zlib

    import numpy as np

    out = dict(_drawn_inputs(seed))
    spreads = {'L0_gnn_bq': (0.0, 0.1),
     'L0_gnn_bk': (0.0, 0.1),
     'L0_gnn_bv': (0.0, 0.1),
     'L1_gnn_b': (0.0, 0.1)}
    factors = {}
    for name, (base, spread) in spreads.items():
        noise = np.random.default_rng([zlib.crc32(name.encode()), seed]).standard_normal(out[name].shape)
        drawn = base * np.exp(spread * noise) if base else spread * noise
        out[name] = jnp.asarray(drawn.astype(out[name].dtype))
    for name, factor in factors.items():
        out[name] = (out[name] * factor).astype(out[name].dtype)
    return out
```

```python
from contextlib import ExitStack

import concourse.bass as bass
from concourse import mybir

ALU = mybir.AluOpType
ACT = mybir.ActivationFunctionType
AX = mybir.AxisListType
F32 = mybir.dt.float32
F16 = mybir.dt.float16
U32 = mybir.dt.uint32

P = 128
LN2 = 0.6931471805599453


def adj_resnorm_kernel(nc, x, adj, wq, bq, wk, wv, bv, w1, b1, a_self, a_neigh, out):
    N, D = x.shape
    H, _, DH = w1.shape
    NT = N // P
    KC = D // P
    CH = 512
    NCH = N // CH
    JB = CH // P
    NG = NT // JB
    NQ = 4
    QW = N // NQ
    SLOTS = 3
    assert D == 512 and N % CH == 0 and H * DH == D and NT % 3 == 2 and NG % 2 == 0

    W_UP = 32.0
    XT_UP = 0.125
    Y_UP = 8.0
    XV_UP = 32.0
    X1_UP = 8.0
    B_UP = 16.0
    P_LOG2 = 14
    HALF_SCALE = 0.5 / float(D) ** 0.5
    NEG_INF = -1.0e10
    EPS = 1.0e-5

    ctx = ExitStack()
    with ctx:
        def sb(name, shape, dt):
            return ctx.enter_context(nc.sbuf_tensor(name, shape, dt))

        def sem(name):
            return ctx.enter_context(nc.semaphore(name))

        def dram(name, shape, dt):
            return nc.dram_tensor(name, shape, dt, kind="Internal").ap()

        xT = sb("xT", [P, 2, KC, N], F16)
        xv = sb("xv", [P, 2, NT, D], F16)
        ring = sb("ring", [P, SLOTS, N], F32)
        wvT = sb("wvT", [P, 2, KC, D], F16)
        w1s = sb("w1s", [P, 2, KC, D], F16)
        yq = sb("yq", [P, 2, KC, P], F16)
        pT = sb("pT", [P, 2, 2, CH], F16)
        post = sb("post", [P, D], F32)
        res = sb("res", [P, D], F32)
        postT = sb("postT", [P, 2, KC, P], F16)
        brow = sb("brow", [P, D], F16)
        sel_v = sb("sel_v", [P, P], F16)
        sel_b = sb("sel_b", [P, P], F16)
        ident = sb("ident", [P, P], F32)
        top2 = sb("top2", [P, NT, 2], F32)
        pick = sb("pick", [P, NT], U32)
        cand = sb("cand", [P, NQ, 8], F32)
        cidx = sb("cidx", [P, NQ, 8], U32)
        gidx = sb("gidx", [P, NQ, 8], F32)
        offs = sb("offs", [P, NQ, 8], F32)
        top8 = sb("top8", [P, 8], F32)
        pickf = sb("pickf", [P, 1], F32)
        u = sb("u", [P, KC, 2 * H], F32)
        c8 = sb("c8", [P, KC], F32)
        bqc = sb("bqc", [P, KC], F32)
        ones = sb("ones", [P, 1], F32)
        eps = sb("eps", [P, 1], F32)
        mhalf = sb("mhalf", [P, 1], F32)
        thr = sb("thr", [P, 1], F32)
        cmax = sb("cmax", [P, NCH], F32)
        rmax = sb("rmax", [P, 1], F32)
        shift = sb("shift", [P, 1], F32)
        sums = sb("sums", [P, NQ], F32)
        rsum = sb("rsum", [P, 1], F32)
        rinv = sb("rinv", [P, 1], F32)
        stats = sb("stats", [P, 6], F32)
        mv = sb("mv", [P, 2], F32)
        ve = sb("ve", [P, 1], F32)
        rstd = sb("rstd", [P, 1], F32)
        flag = sb("flag", [1, 1], U32)

        wf = ring[:, 0, :].rearrange("p (a c n) -> p a c n", a=2, c=KC)
        m16 = ring[:, 1, 0:N // 2].bitcast(F16).rearrange("p (a c n) -> p a c n", a=2, c=KC)
        xs = [ring[:, 1, N // 2:N].rearrange("p (j n) -> p j n", j=JB),
              ring[:, 2, 0:N // 2].rearrange("p (j n) -> p j n", j=JB)]
        w16 = ring[:, 2, :].bitcast(F16).rearrange("p (w a c n) -> p w a c n", w=2, a=2, c=KC)
        ybuf = ring[:, 2, N // 2:N].bitcast(F16).rearrange("p (j a c n) -> p j a c n", j=JB, a=2, c=KC)
        wvf = xv[:, 0, 24:32, :].bitcast(F32).rearrange("p (c b) n -> p c (b n)", c=KC)
        w1f = xv[:, 1, 24:32, :].bitcast(F32).rearrange("p (c b) n -> p c (b n)", c=KC)
        prod = [xv[:, a, 16:24, :].bitcast(F32).rearrange("p (c b) n -> p c (b n)", c=KC) for a in range(2)]
        ab = [pT[:, s, :, :].bitcast(F32).rearrange("p a n -> p (a n)") for s in range(2)]
        yf = [res, post]
        onesq = xv[:, 0, 12, 0:2 * P].bitcast(F32)
        usq = xv[:, 0, 13, 0:2 * KC * 2 * H].bitcast(F32)
        brf = yq[:, :, :, :].bitcast(F32).rearrange("p a c n -> p (a c n)")
        brh = postT[:, 0, :, :].rearrange("p c n -> p (c n)")
        brl = postT[:, 1, :, :].rearrange("p c n -> p (c n)")

        S = [ctx.enter_context(nc.psum_tensor(f"S{k}", [P, CH], F32)) for k in range(3)]
        PT = [ctx.enter_context(nc.psum_tensor(f"PT{k}", [P, CH], F32)) for k in range(2)]
        O = ctx.enter_context(nc.psum_tensor("O", [P, CH], F32))
        T = ctx.enter_context(nc.psum_tensor("T", [P, CH], F32))
        VF = ctx.enter_context(nc.psum_tensor("VF", [P, CH], F32))

        y_d = dram("y_scratch", [N, 2 * KC * P], F16)
        x1_d = dram("x1_scratch", [N, D], F32)
        f_d = dram("feats_scratch", [N, D], F32)

        wqk_in, wv_in, w1_in, small_in, a_in = map(sem, ("wqk_in", "wv_in", "w1_in", "small_in", "a_in"))
        xs_in = [sem("xs_in0"), sem("xs_in1")]
        const_set, brf_zero = sem("const_set"), sem("brf_zero")
        sel_set = sem("sel_set")
        ident_zero, ident_set = sem("ident_zero"), sem("ident_set")
        w_hi, w_lo = sem("w_hi"), sem("w_lo")
        m_ready, m_hi, m_lo = sem("m_ready"), sem("m_hi"), sem("m_lo")
        c_ready, c_set = sem("c_ready"), sem("c_set")
        wvT_ready, wvT_hi, wvT_lo = sem("wvT_ready"), sem("wvT_hi"), sem("wvT_lo")
        w1_hi, w1_lo = sem("w1_hi"), sem("w1_lo")
        br_hi, br_lo, br_set = sem("br_hi"), sem("br_lo"), sem("br_set")
        prod_set, u_set, usq_set, usum_ready, thr_set = map(sem, ("prod_set", "u_set", "usq_set", "usum_ready", "thr_set"))
        xt_ready, xt_hi, xt_lo = sem("xt_ready"), sem("xt_hi"), sem("xt_lo")
        yp_ready, y_f, y_hi, y_lo = sem("yp_ready"), sem("y_f"), sem("y_hi"), sem("y_lo")
        xv_hi, xv_lo = sem("xv_hi"), sem("xv_lo")
        y_out = sem("y_out")
        adj_in = sem("adj_in")
        y_in, res_in, x1_out, f_out = map(sem, ("y_in", "res_in", "x1_out", "f_out"))
        s_ready, s_used = sem("s_ready"), sem("s_used")
        rmax_set, shift_set = sem("rmax_set"), sem("shift_set")
        p_ready, rsum_set, rinv_set = sem("p_ready"), sem("rsum_set"), sem("rinv_set")
        pt_ready, pt_hi, pt_lo, pv_done = map(sem, ("pt_ready", "pt_hi", "pt_lo", "pv_done"))
        ctx_set, ctxT_ready, ctxT_hi, ctxT_lo = map(sem, ("ctx_set", "ctxT_ready", "ctxT_hi", "ctxT_lo"))
        v_ready, h_set, stats_set, mv_set, ve_set, rstd_set = map(
            sem, ("v_ready", "h_set", "stats_set", "mv_set", "ve_set", "rstd_set"))
        x1_set, x1T_ready, x1T_hi, x1T_lo = map(sem, ("x1_set", "x1T_ready", "x1T_hi", "x1T_lo"))
        f_ready, f_set = sem("f_ready"), sem("f_set")
        cand_set, cidx_set = sem("cand_set"), sem("cidx_set")
        top_set, gidx_set, pickf_set, scan_set = map(sem, ("top_set", "gidx_set", "pickf_set", "scan_set"))
        ok_chain, count_ready, flag_set = sem("ok_chain"), sem("count_ready"), sem("flag_set")
        NE = NT // JB
        x1r_in = [sem(f"x1r_in{e}") for e in range(NE)]
        got_in = [sem(f"got_in{e}") for e in range(NE)]
        e_sum, e_stats, e_mv, e_sd, e_chain, e_rstd, e_out, out_done = map(
            sem, ("e_sum", "e_stats", "e_mv", "e_sd", "e_chain", "e_rstd", "e_out", "out_done"))

        x1r = xT[:, :, :, :].bitcast(F32).rearrange("p a c n -> p (a c n)").rearrange("p (t d) -> p t d", d=D)
        got = xv[:, :, :, :].bitcast(F32).rearrange("p a t n -> p (a t n)").rearrange("p (t d) -> p t d", d=D)
        end = ring[:, 2, :]
        e_st = end[:, 0:NT * 6].rearrange("p (t s) -> p t s", s=6)
        e_mean = end[:, 256:256 + 2 * NT].rearrange("p (t s) -> p t s", s=2)
        e_s = end[:, 384:384 + NT]
        e_r = end[:, 448:448 + NT]
        e_t = end[:, 512:512 + NT]
        e_nm = end[:, 576:576 + NT]
        okw = ring[:, 2, 1024:1024 + 8 * NT]

        g_adj, g_z, g_nb = ring[:, 0, :], ring[:, 1, :], ring[:, 2, :]
        g_feats, g_out = x1r, got
        g_p = [wvT[:, a, :, :].bitcast(F32).rearrange("p c n -> p (c n)")[:, 0:CH] for a in range(2)]
        g_xT = w1s[:, 0, :, :].bitcast(F32).rearrange("p c n -> p (c n)")[:, 0:D]
        g_es = w1s[:, 1, :, :].bitcast(F32).rearrange("p c n -> p (c n)")[:, 0:NT * H]\
            .rearrange("p (t h) -> p t h", h=H)
        g_enT = ring[0:H, 0, :]
        g_row = brow[:, 0:2 * DH].bitcast(F32)
        en_d = dram("e_neigh_scratch", [H, N], F32)
        (gx_in, gT_ready, gT_copied, ge_ready, ge_copied, gen_out, gf_in, gnb_in, ga_in, g_mask, g_log, g_z_set,
         g_shift, g_exp, g_tr, g_pc, g_mm, g_o, g_inv, gh_set, gh_stats, gh_mv, gh_ve, gh_rstd, gh_fin, gh_out
         ) = (sem(f"general_{name}") for name in (
             "x1_in", "x1T_ready", "x1T_copied", "e_ready", "e_copied", "e_neigh_out", "feats_in", "neigh_in",
             "adj_in", "mask", "logits", "z", "shift", "exp", "transposed", "p_copied", "multiplied", "out_set",
             "inv", "h", "stats", "mv", "ve", "rstd", "final", "out"))

        def if_general(eng, path, from_one=()):
            eng.wait_ge(flag_set, 1)
            with eng.register("proven") as proven:
                eng.reg_load(proven, flag[0:1, 0:1])
                with eng.If_ne(proven, N):
                    eng.wait_ge(out_done, 16 * NE)
                    for semaphore in from_one:
                        eng.sem_inc(semaphore, 1)
                    path()

        block = ctx.enter_context(nc.Block())

        def run_steps(eng, step, rounds, first=2):
            for s in range(first):
                step(s, s)
            with eng.Fori(0, rounds) as i:
                for k in range(3):
                    step(i * 3 + (first + k), first + k)
            for s in range(first + 3 * rounds, NT + 2):
                step(s, s)

        def run_groups(eng, transposed, queries):
            transposed(0, 0)
            transposed(1, 1)
            queries(0, 0)
            with eng.Fori(0, NG // 2 - 1) as i:
                for k in range(2):
                    transposed(i * 2 + (k + 2), k + 2)
                    queries(i * 2 + (k + 1), k + 1)
            queries(NG - 1, NG - 1)


        @block.sync
        def _(sp):
            yq_flat = yq[:, :, :, :].rearrange("p a c n -> p (a c n)")
            sp.dma_start(wf[:, 0], wq.rearrange("(c p) n -> p c n", p=P)).then_inc(wqk_in, 16)
            sp.dma_start(wf[:, 1], wk.rearrange("(c p) n -> p c n", p=P)).then_inc(wqk_in, 16)

            def load_x(g, k):
                sp.dma_start(xs[k % 2], x[bass.ds(g * (JB * P), JB * P), :]
                             .rearrange("(j p) n -> p j n", p=P)).then_inc(xs_in[k % 2], 16)

            load_x(0, 0)
            sp.dma_start(wvf, wv.rearrange("(c p) n -> p c n", p=P)).then_inc(wv_in, 16)
            for kc in range(KC):
                sp.dma_start(w1f[:, kc, :].rearrange("p (h d) -> p h d", h=H),
                             w1[:, kc * P:(kc + 1) * P, :].rearrange("h p d -> p h d")).then_inc(w1_in, 16)
            sp.dma_start(bqc[:, :], bq.rearrange("(c p) -> p c", p=P), allow_slow_non_contiguous=True).then_inc(small_in, 16)
            sp.wait_ge(brf_zero, 1)
            b1_row = b1.rearrange("h d -> (h d)").rearrange("(a n) -> a n", a=1)
            bv_row = bv.rearrange("(a n) -> a n", a=1)
            for row, vec in ((0, bv_row), (32, bv_row), (64, b1_row), (96, b1_row)):
                sp.dma_start(brf[row:row + 1, :], vec).then_inc(small_in, 16)
            for k, a in enumerate((a_self, a_neigh)):
                sp.dma_start(ab[k], a.rearrange("h d -> (h d)").rearrange("(a n) -> a n", a=1)
                             .broadcast_to([P, D])).then_inc(a_in, 16)
            sp.wait_ge(m_ready, KC)
            load_x(1, 1)
            sp.wait_ge(c_ready, 1)
            sp.wait_ge(w_lo, 2)
            sp.dma_start(ring[:, 0, :], adj[0:P, :]).then_inc(adj_in, 16)

            def store_queries(g):
                sp.wait_ge(y_lo, (g + 1) * KC)
                sp.dma_start(y_d[bass.ds(g * (JB * P), JB * P), :].rearrange("(j p) m -> p j m", p=P),
                             ybuf.rearrange("p j a c n -> p j (a c n)")).then_inc(y_out, 16)

            with sp.Fori(0, NG // 2 - 1) as i:
                for k in range(2):
                    g = i * 2 + k
                    sp.wait_ge(xt_ready, (g + 1) * KC)
                    sp.wait_ge(xv_hi, g + 1)
                    sp.wait_ge(xv_lo, g + 1)
                    load_x(g + 2, k)
                    store_queries(g)
            store_queries(NG - 2)
            store_queries(NG - 1)
            sp.wait_ge(y_out, 16 * NG)
            sp.dma_start(yq_flat, y_d[0:P, :]).then_inc(y_in, 16)
            sp.wait_ge(yp_ready, KC * NG)
            sp.wait_ge(xv_hi, NG)
            sp.wait_ge(xv_lo, NG)
            sp.wait_ge(adj_in, 16)
            sp.dma_start(ring[:, 1, :], adj[P:2 * P, :]).then_inc(adj_in, 16)

            def step(s, c):
                if 1 <= c < NT - 1:
                    if c >= 2:
                        sp.wait_ge(pt_ready, (s - 1) * NCH)
                    sp.wait_ge(adj_in, s * 16 + 16)
                    sp.dma_start(ring[:, (c + 1) % SLOTS, :], adj[bass.ds((s + 1) * P, P), :]
                                 ).then_inc(adj_in, 16)
                if c >= 2:
                    sp.wait_ge(x1_set, s - 1)
                    sp.dma_start(x1_d[bass.ds((s - 2) * P, P), :], res[:, :]).then_inc(x1_out, 16)
                if c < NT - 1:
                    sp.wait_ge(s_ready, (s + 1) * NCH)
                    sp.dma_start(yq_flat, y_d[bass.ds((s + 1) * P, P), :]).then_inc(y_in, 16)
                if 1 <= c <= NT:
                    if c >= 2:
                        sp.wait_ge(x1_out, (s - 1) * 16)
                        sp.wait_ge(x1T_ready, s - 1)
                    else:
                        sp.wait_ge(y_lo, KC * NG)
                    sp.dma_start(res[:, :], x[bass.ds((s - 1) * P, P), :]).then_inc(res_in, 16)
                if c >= 2:
                    sp.wait_ge(f_set, s - 1)
                    sp.dma_start(f_d[bass.ds((s - 2) * P, P), :], post[:, :]).then_inc(f_out, 16)
                if c == NT:
                    sp.wait_ge(s_ready, NT * NCH)
                    for e in range(NE - 1):
                        load_x1(e)

            def load_x1(e):
                sp.dma_start(x1r[:, e * JB:(e + 1) * JB, :],
                             x1_d[e * JB * P:(e + 1) * JB * P, :].rearrange("(j p) n -> p j n", p=P)
                             ).then_inc(x1r_in[e], 16)

            run_steps(sp, step, NT // 3 - 1)
            sp.wait_ge(x1_out, 16 * NT)
            load_x1(NE - 1)
            for e in range(NE):
                sp.wait_ge(e_out, (e + 1) * JB)
                sp.dma_start(out[e * JB * P:(e + 1) * JB * P, :].rearrange("(j p) n -> p j n", p=P),
                             got[:, e * JB:(e + 1) * JB, :]).then_inc(out_done, 16)
            sp.wait_ge(out_done, 16 * NE)
            sp.wait_ge(f_out, 16 * NT)

            def general():
                with sp.Fori(0, NT) as t:
                    sp.wait_ge(gT_ready, t + 1)
                    sp.dma_start(res[:, :], x1_d[bass.ds(t * P, P), :]).then_inc(gx_in, 16)
                sp.dma_start(g_feats, f_d.rearrange("(t p) n -> p t n", p=P)).then_inc(gf_in, 16)
                sp.wait_ge(ge_copied, 2 * NT + 1)
                sp.dma_start(en_d, g_enT).then_inc(gen_out, 16)
                sp.wait_ge(gen_out, 16)
                with sp.Fori(0, H) as h:
                    sp.wait_ge(g_z_set, h * NT + 1)
                    sp.dma_start(g_nb, en_d[bass.ds(h, 1), :].broadcast_to([P, N])).then_inc(gnb_in, 16)
                    with sp.Fori(0, NT) as t:
                        sp.wait_ge(g_log, h * NT + t + 1)
                        sp.dma_start(g_adj, adj[bass.ds(t * P, P), :]).then_inc(ga_in, 16)
                sp.dma_start(res[:, :], x1_d[0:P, :]).then_inc(gx_in, 16)
                with sp.Fori(0, NT - 1) as t:
                    sp.wait_ge(gh_fin, t + 1)
                    sp.dma_start(out[bass.ds(t * P, P), :], res[:, :]).then_inc(gh_out, 16)
                    sp.wait_ge(gh_out, t * 16 + 16)
                    sp.dma_start(res[:, :], x1_d[bass.ds((t + 1) * P, P), :]).then_inc(gx_in, 16)
                sp.wait_ge(gh_fin, NT)
                sp.dma_start(out[N - P:N, :], res[:, :]).then_inc(gh_out, 16)
                sp.wait_ge(gh_out, 16 * NT)

            if_general(sp, general)

        @block.gpsimd
        def _(pool):
            pool.memset(brf[:, :], 0.0).then_inc(brf_zero, 1)
            pool.memset(ident[:, :], 0.0).then_inc(ident_zero, 1)
            pool.wait_ge(ident_zero, 1)
            pool.affine_select(out=ident[:, :], in_=ident[:, :], compare_op=ALU.not_equal, fill=1.0,
                               base=0, pattern=[[-1, P]], channel_multiplier=1).then_inc(ident_set, 1)
            pool.memset(ones[:, :], 1.0)
            pool.memset(onesq, 1.0)
            pool.memset(eps[:, :], EPS)
            pool.memset(mhalf[:, :], -0.5)
            for q in range(NQ):
                last = pool.memset(offs[:, q, :], float(q * QW))
            last.then_inc(const_set, 1)
            pool.wait_ge(w1_in, 16 * KC)
            pool.wait_ge(a_in, 32)
            for k in range(2):
                for kc in range(KC):
                    pool.tensor_tensor(prod[k][:, kc, :], w1f[:, kc, :], ab[k], ALU.mult).then_inc(prod_set, 1)

            def step(s, c):
                if c >= 2:
                    pool.wait_ge(mv_set, s - 1)
                    pool.tensor_tensor(ve[:, :], mv[:, 1:2], eps[:, :], ALU.add).then_inc(ve_set, 1)
                    pool.wait_ge(ve_set, s - 1)
                    pool.tensor_tensor(rstd[:, :], ve[:, :], mhalf[:, :], ALU.pow).then_inc(rstd_set, 1)

            with pool.Fori(2, NT + 2) as s:
                step(s, 2)

            pool.wait_ge(f_out, 16 * NT)
            pool.wait_ge(scan_set, 2 * NT)
            for t in range(NT):
                pool.indirect_dma_start(out=got[:, t, :], out_offset=None, in_=f_d,
                                        in_offset=bass.IndirectOffsetOnAxis(ap=pick[:, t:t + 1], axis=0)
                                        ).then_inc(got_in[t // JB], 16)

            def general():
                with pool.Fori(0, NT) as t:
                    pool.wait_ge(gh_mv, t + 1)
                    pool.tensor_tensor(ve[:, :], mv[:, 1:2], eps[:, :], ALU.add).then_inc(gh_ve, 1)
                    pool.wait_ge(gh_ve, t + 1)
                    pool.tensor_tensor(rstd[:, :], ve[:, :], mhalf[:, :], ALU.pow).then_inc(gh_rstd, 1)

            if_general(pool, general)

        @block.tensor
        def _(pe):
            Y = [S[0], S[1], S[2], VF]
            X = [PT[0], PT[1], O, T]

            def split_product(psum, sta, mov, n, first=True, last=True):
                for k in range(n):
                    for a, b in ((0, 0), (0, 1), (1, 0)):
                        mm = pe.matmul(psum, sta(a, k), mov(b, k), start=(first and k == 0 and a + b == 0),
                                       stop=(last and k == n - 1 and a == 1))
                return mm

            pe.wait_ge(w_hi, 2)
            pe.wait_ge(w_lo, 2)
            for ic in range(KC):
                split_product(Y[ic][:, :], lambda a, o: w16[:, 0, a, o, ic * P:(ic + 1) * P],
                              lambda b, o: w16[:, 1, b, o, :], KC).then_inc(m_ready, 1)
            pe.wait_ge(small_in, 16 * 5)
            for jc in range(KC):
                for o in range(KC):
                    mm = pe.matmul(T[:, jc:jc + 1], wf[:, 1, o, jc * P:(jc + 1) * P], bqc[:, o:o + 1],
                                   start=(o == 0), stop=(o == KC - 1))
            mm.then_inc(c_ready, 1)
            pe.wait_ge(wv_in, 16)
            pe.wait_ge(ident_set, 1)
            pe.wait_ge(c_set, 1)
            for ic in range(KC):
                for o in range(KC):
                    mm = pe.transpose(X[ic][:, o * P:(o + 1) * P], wvf[:, o, ic * P:(ic + 1) * P], ident[:, :])
                mm.then_inc(wvT_ready, 1)
            pe.wait_ge(usq_set, 1)
            pe.wait_ge(const_set, 1)
            pe.wait_ge(wvT_lo, KC)
            pe.matmul(PT[0][:, 0:1], onesq, rsum[:, :], start=True, stop=True).then_inc(usum_ready, 1)
            pe.wait_ge(thr_set, 1)

            def transposed(g, c):
                pe.wait_ge(xs_in[c % 2], (g - c % 2) * 8 + 16)
                for kc in range(KC):
                    if c >= 1:
                        pe.wait_ge(xt_lo, g * KC + (kc + 1 - KC))
                    for j in range(JB):
                        mm = pe.transpose(X[kc][:, j * P:(j + 1) * P], xs[c % 2][:, j, kc * P:(kc + 1) * P],
                                          ident[:, :])
                    mm.then_inc(xt_ready, 1)

            def queries(g, c):
                pe.wait_ge(xt_lo, g * KC + KC)
                if c == 0:
                    pe.wait_ge(m_lo, KC)
                for jc in range(KC):
                    if c >= 1:
                        pe.wait_ge(y_f, g * KC + (jc + 1 - KC))
                    split_product(Y[jc][:, :], lambda a, k: m16[:, a, k, jc * P:(jc + 1) * P],
                                  lambda b, k: xT[:, b, k, bass.ds(g * CH, CH)], KC).then_inc(yp_ready, 1)

            run_groups(pe, transposed, queries)

            def scores(s, c, k):
                if k == 0:
                    pe.wait_ge(y_in, s * 16 + 16)
                    if c == 0:
                        pe.wait_ge(y_f, KC * NG)
                n = c * NCH + k
                if n >= 3:
                    pe.wait_ge(s_used, s * NCH + (k - 2))
                split_product(S[n % 3][:, :], lambda a, kc: yq[:, a, kc, :],
                              lambda b, kc: xT[:, b, kc, k * CH:(k + 1) * CH], KC).then_inc(s_ready, 1)

            def transpose_exponentials(t, c, g):
                pe.wait_ge(p_ready, t * NQ + (g // 2 + 1))
                if c * NCH + g >= 2:
                    pe.wait_ge(pt_lo, t * NCH + (g - 1))
                for j in range(JB):
                    m = (g * JB + j) * P
                    mm = pe.transpose(PT[g % 2][:, j * P:(j + 1) * P], ring[:, c % SLOTS, m:m + P], ident[:, :])
                mm.then_inc(pt_ready, 1)

            def values(t, c, g):
                pe.wait_ge(pt_lo, t * NCH + (g + 1))
                if g == 0 and c >= 1:
                    pe.wait_ge(ctx_set, t)
                split_product(O[:, :], lambda a, j: pT[:, g % 2, a, j * P:(j + 1) * P],
                              lambda b, j: xv[:, b, g * JB + j, :], JB, g == 0, g == NCH - 1).then_inc(pv_done, 1)

            def transpose_ctx(t):
                pe.wait_ge(ctx_set, t + 1)
                for kc in range(KC):
                    mm = pe.transpose(T[:, kc * P:(kc + 1) * P], post[:, kc * P:(kc + 1) * P], ident[:, :])
                mm.then_inc(ctxT_ready, 1)

            def project_values(t, c):
                pe.wait_ge(ctxT_lo, t + 1)
                if c >= 1:
                    pe.wait_ge(f_set, t)
                pe.matmul(VF[:, :], sel_v[:, :], brow[:, :], start=True, stop=False)
                split_product(VF[:, :], lambda a, k: postT[:, a, k, :], lambda b, k: wvT[:, b, k, :], KC, False
                              ).then_inc(v_ready, 1)

            def transpose_x1(t):
                pe.wait_ge(x1_set, t + 1)
                for kc in range(KC):
                    mm = pe.transpose(T[:, kc * P:(kc + 1) * P], res[:, kc * P:(kc + 1) * P], ident[:, :])
                mm.then_inc(x1T_ready, 1)

            def feats(t):
                pe.wait_ge(x1T_lo, t + 1)
                pe.matmul(VF[:, :], sel_b[:, :], brow[:, :], start=True, stop=False)
                split_product(VF[:, :], lambda a, k: postT[:, a, k, :], lambda b, k: w1s[:, b, k, :], KC, False
                              ).then_inc(f_ready, 1)

            def step(s, c):
                score, value, follow = c < NT, 1 <= c <= NT, c >= 2
                for k in range(NCH):
                    if score:
                        scores(s, c, k)
                    if follow and k == 1:
                        transpose_ctx(s - 2)
                    if follow and k == 3:
                        project_values(s - 2, c - 2)
                    if follow and k == 6:
                        transpose_x1(s - 2)
                    if value and k in (4, 5):
                        transpose_exponentials(s - 1, c - 1, k - 4)
                for g in range(NCH):
                    if value and g + 2 < NCH:
                        transpose_exponentials(s - 1, c - 1, g + 2)
                    if value:
                        values(s - 1, c - 1, g)
                    if follow and g == 1:
                        feats(s - 2)

            pe.wait_ge(br_set, 1)
            pe.wait_ge(sel_set, 1)
            pe.wait_ge(w1_lo, 1)
            run_steps(pe, step, NT // 3)
            pe.wait_ge(ok_chain, 8)
            pe.matmul(S[0][0:1, 0:1], okw[:, 0:1], ones[:, :], start=True, stop=True).then_inc(count_ready, 1)

            def general():
                with pe.Fori(0, NT) as t:
                    pe.wait_ge(gx_in, t * 16 + 16)
                    pe.wait_ge(gT_copied, t + 1)
                    for kc in range(KC):
                        mm = pe.transpose(T[:, kc * P:(kc + 1) * P], res[:, kc * P:(kc + 1) * P], ident[:, :])
                    mm.then_inc(gT_ready, 1)
                    pe.wait_ge(gT_copied, t + 2)
                    pe.wait_ge(ge_copied, t * 2 + 1)
                    for kc in range(KC):
                        pe.matmul(S[0][0:H, 0:P], u[:, kc, H:2 * H], g_xT[:, kc * P:(kc + 1) * P],
                                  start=(kc == 0), stop=(kc == KC - 1))
                    for kc in range(KC):
                        mm = pe.matmul(S[1][:, 0:H], g_xT[:, kc * P:(kc + 1) * P], u[:, kc, 0:H],
                                       start=(kc == 0), stop=(kc == KC - 1))
                    mm.then_inc(ge_ready, 1)
                pe.wait_ge(gf_in, 16)
                with pe.Fori(0, H) as h:
                    with pe.Fori(0, NT) as t:
                        n = h * NT + t
                        pe.wait_ge(g_exp, n + 1)
                        for g in range(NCH):
                            pe.wait_ge(g_pc, n * NCH + max(g - 1, 0) + 1)
                            for j in range(JB):
                                m = (g * JB + j) * P
                                mm = pe.transpose(PT[g % 2][:, j * P:(j + 1) * P], g_z[:, m:m + P], ident[:, :])
                            mm.then_inc(g_tr, 1)
                            pe.wait_ge(g_pc, n * NCH + (g + 1) + 1)
                            if g == 0:
                                pe.wait_ge(g_o, n + 1)
                            for j in range(JB):
                                mm = pe.matmul(O[:, 0:DH], g_p[g % 2][:, j * P:(j + 1) * P],
                                               g_feats[:, g * JB + j, bass.ds(h * DH, DH)],
                                               start=(g == 0 and j == 0), stop=(g == NCH - 1 and j == JB - 1))
                            mm.then_inc(g_mm, 1)

            if_general(pe, general, (gT_ready, ge_ready, g_tr, g_mm))

        @block.scalar
        def _(act):
            Y = [S[0], S[1], S[2], VF]
            X = [PT[0], PT[1], O, T]

            def scaled(dst, src, scale):
                return nc.scalar.activation(dst, src, ACT.Copy, scale=scale)

            act.wait_ge(wqk_in, 32)
            for w in range(2):
                scaled(w16[:, w, 0], wf[:, w], W_UP).then_inc(w_hi, 1)
            for ic in range(KC):
                act.wait_ge(m_ready, ic + 1)
                scaled(m16[:, 0, ic, :], Y[ic][:, :], 1.0 / W_UP).then_inc(m_hi, 1)
            for ic in range(KC):
                act.wait_ge(wvT_ready, ic + 1)
                scaled(wvT[:, 0, ic, :], X[ic][:, :], W_UP).then_inc(wvT_hi, 1)
            act.wait_ge(w1_in, 16 * KC)
            scaled(w1s[:, 0], w1f, W_UP).then_inc(w1_hi, 1)

            def transposed(g, c):
                for kc in range(KC):
                    act.wait_ge(xt_ready, g * KC + (kc + 1))
                    scaled(xT[:, 0, kc, bass.ds(g * CH, CH)], X[kc][:, :], XT_UP).then_inc(xt_hi, 1)
                if c == 0:
                    act.wait_ge(w1_lo, 1)
                    act.wait_ge(usum_ready, 1)
                act.wait_ge(xs_in[c % 2], (g - c % 2) * 8 + 16)
                scaled(xv[:, 0, bass.ds(g * JB, JB), :], xs[c % 2], XV_UP).then_inc(xv_hi, 1)

            def queries(g, c):
                if c == 0:
                    act.wait_ge(c_set, 1)
                for jc in range(KC):
                    act.wait_ge(yp_ready, g * KC + (jc + 1))
                    if c * KC + jc >= 2:
                        act.wait_ge(y_lo, g * KC + (jc - 1))
                    nc.scalar.activation(yf[jc % 2][:, :], Y[jc][:, :], ACT.Identity, bias=c8[:, jc:jc + 1],
                                         scale=HALF_SCALE * Y_UP / (W_UP * XT_UP)).then_inc(y_f, 1)

            run_groups(act, transposed, queries)

            def exponentials(s, c, q):
                if q == 0:
                    act.wait_ge(shift_set, s + 1)
                    if c >= 1:
                        act.wait_ge(rsum_set, s)
                row = ring[:, c % SLOTS, q * QW:(q + 1) * QW]
                nc.scalar.activation(row, row, ACT.Exp, bias=shift[:, :], scale=2.0,
                                     accum_out=sums[:, q:q + 1]).then_inc(p_ready, 1)

            def exponentials_hi(t, c, g):
                act.wait_ge(pt_ready, t * NCH + (g + 1))
                if c * NCH + g >= 2:
                    act.wait_ge(pv_done, t * NCH + (g - 1))
                scaled(pT[:, g % 2, 0, :], PT[g % 2][:, :], 1.0).then_inc(pt_hi, 1)

            def step(s, c):
                score, value, follow = c < NT, 1 <= c <= NT, c >= 2
                if follow:
                    act.wait_ge(ctxT_ready, s - 1)
                    if c >= 3:
                        act.wait_ge(f_ready, s - 2)
                    scaled(postT[:, 0].rearrange("p c n -> p (c n)"), T[:, :], 1.0).then_inc(ctxT_hi, 1)
                if value:
                    for g in range(2):
                        exponentials_hi(s - 1, c - 1, g)
                if follow:
                    act.wait_ge(x1T_ready, s - 1)
                    scaled(postT[:, 0].rearrange("p c n -> p (c n)"), T[:, :], X1_UP).then_inc(x1T_hi, 1)
                for g in range(2, NCH):
                    if score and g - 2 < NQ:
                        exponentials(s, c, g - 2)
                    if value:
                        exponentials_hi(s - 1, c - 1, g)
                    if follow and g == 4:
                        act.wait_ge(f_ready, s - 1)
                        scaled(post[:, :], VF[:, :], 1.0 / (W_UP * X1_UP)).then_inc(f_set, 1)
                if value:
                    act.wait_ge(pv_done, s * NCH)
                    act.wait_ge(rinv_set, s)
                    if c >= 2:
                        act.wait_ge(f_out, s * 16 - 16)
                    nc.scalar.activation(post[:, :], O[:, :], ACT.Identity, scale=rinv[:, :]).then_inc(ctx_set, 1)

            run_steps(act, step, NT // 3)

            def normalise(e):
                act.wait_ge(e_rstd, e + 1)
                for t in range(e * JB, (e + 1) * JB):
                    nc.scalar.activation(got[:, t, :], got[:, t, :], ACT.Identity, bias=e_nm[:, t:t + 1],
                                         scale=e_r[:, t:t + 1]).then_inc(e_out, 1)

            for e in range(NE):
                tiles = slice(e * JB, (e + 1) * JB)
                act.wait_ge(e_mv, (e + 1) * JB)
                nc.scalar.activation(e_s[:, tiles], e_mean[:, tiles, 1], ACT.Sqrt, bias=eps[:, :]).then_inc(e_sd, 1)
                if e >= 1:
                    normalise(e - 1)
            normalise(NE - 1)

            def general():
                with act.Fori(0, NT) as t:
                    act.wait_ge(gT_ready, t + 2)
                    act.wait_ge(ge_ready, t + 1)
                    scaled(g_xT, T[:, :], 1.0).then_inc(gT_copied, 1)
                with act.Fori(0, H) as h:
                    with act.Fori(0, NT) as t:
                        n = h * NT + t
                        act.wait_ge(g_shift, n + 1)
                        nc.scalar.activation(g_z, g_z, ACT.Exp, bias=shift[:, :], scale=1.0,
                                             accum_out=rsum[:, :]).then_inc(g_exp, 1)
                        for g in range(NCH):
                            act.wait_ge(g_tr, n * NCH + (g + 1) + 1)
                            act.wait_ge(g_mm, n * NCH + max(g - 1, 0) + 1)
                            scaled(g_p[g % 2], PT[g % 2][:, :], 1.0).then_inc(g_pc, 1)

            if_general(act, general, (gT_copied, g_pc))

        @block.vector
        def _(dve):
            Y = [S[0], S[1], S[2], VF]
            X = [PT[0], PT[1], O, T]

            def lo_part(dst, src, scale, hi):
                return dve.scalar_tensor_tensor(out=dst, in0=src, scalar=scale, in1=hi, op0=ALU.mult,
                                                op1=ALU.subtract)

            dve.memset(sel_v[0:64, :], W_UP * XV_UP / B_UP)
            dve.memset(sel_v[64:P, :], 0.0)
            dve.memset(sel_b[0:64, :], 0.0)
            dve.memset(sel_b[64:P, :], W_UP * X1_UP / B_UP).then_inc(sel_set, 1)

            def wait_apart(semaphore, value):
                dve.wait_ge(semaphore, value)
                dve.nop(nofuse=True)

            for w in range(2):
                dve.wait_ge(w_hi, w + 1)
                lo_part(w16[:, w, 1], wf[:, w], W_UP, w16[:, w, 0]).then_inc(w_lo, 1)
            for ic in range(KC):
                dve.wait_ge(m_hi, ic + 1)
                lo_part(m16[:, 1, ic, :], Y[ic][:, :], 1.0 / W_UP, m16[:, 0, ic, :]).then_inc(m_lo, 1)
            dve.wait_ge(c_ready, 1)
            dve.tensor_scalar(c8[:, :], T[:, 0:KC], Y_UP * HALF_SCALE, None, ALU.mult).then_inc(c_set, 1)
            for ic in range(KC):
                dve.wait_ge(wvT_hi, ic + 1)
                lo_part(wvT[:, 1, ic, :], X[ic][:, :], W_UP, wvT[:, 0, ic, :]).then_inc(wvT_lo, 1)
            dve.wait_ge(small_in, 16 * 5)
            dve.tensor_scalar(brh, brf, B_UP, None, ALU.mult).then_inc(br_hi, 1)
            dve.wait_ge(br_hi, 1)
            lo_part(brl, brf, B_UP, brh).then_inc(br_lo, 1)
            dve.wait_ge(br_lo, 1)
            for k in range(4):
                last = dve.tensor_copy(brow[32 * k:32 * k + 32, :], (brl if k % 2 else brh)[32 * k:32 * k + 32, :])
            last.then_inc(br_set, 1)
            dve.wait_ge(w1_hi, 1)
            lo_part(w1s[:, 1], w1f, W_UP, w1s[:, 0]).then_inc(w1_lo, 1)
            for k in range(2):
                dve.wait_ge(prod_set, (k + 1) * KC)
                dve.tensor_reduce(u[:, :, k * H:(k + 1) * H], prod[k].rearrange("p c (h d) -> p c h d", h=H),
                                  AX.X, ALU.add).then_inc(u_set, 1)
            dve.wait_ge(u_set, 2)
            uf = u[:, :, :].rearrange("p c h -> p (c h)")
            dve.tensor_tensor_reduce(out=usq, in0=uf, in1=uf, scale=1.0, scalar=0.0, op0=ALU.mult,
                                     op1=ALU.add, accum_out=rsum[:, :]).then_inc(usq_set, 1)
            dve.wait_ge(usum_ready, 1)
            dve.tensor_scalar(thr[:, :], PT[0][:, 0:1], 64.0, 64.0 + 200.0, ALU.mult, ALU.add).then_inc(thr_set, 1)

            def transposed(g, c):
                for kc in range(KC):
                    dve.wait_ge(xt_hi, g * KC + (kc + 1))
                    cols = bass.ds(g * CH, CH)
                    lo_part(xT[:, 1, kc, cols], X[kc][:, :], XT_UP, xT[:, 0, kc, cols]).then_inc(xt_lo, 1)
                dve.wait_ge(xv_hi, g + 1)
                tiles = bass.ds(g * JB, JB)
                lo_part(xv[:, 1, tiles, :].rearrange("p t n -> p (t n)"), xs[c % 2].rearrange("p t n -> p (t n)"),
                        XV_UP, xv[:, 0, tiles, :].rearrange("p t n -> p (t n)")).then_inc(xv_lo, 1)

            def queries(g, c):
                for jc in range(KC):
                    dve.wait_ge(y_f, g * KC + (jc + 1))
                    if jc == 0 and c >= 1:
                        dve.wait_ge(y_out, g * 16)
                    src = yf[jc % 2][:, :].rearrange("p (j n) -> p j n", j=JB)
                    dve.tensor_copy(ybuf[:, :, 0, jc, :], src).then_inc(y_hi, 1)
                    dve.wait_ge(y_hi, g * KC + (jc + 1))
                    dve.tensor_tensor(ybuf[:, :, 1, jc, :], src, ybuf[:, :, 0, jc, :], ALU.subtract).then_inc(y_lo, 1)

            run_groups(dve, transposed, queries)

            def scan(t, c, q):
                if q == 0:
                    wait_apart(adj_in, t * 16 + 16)
                part = ring[:, c % SLOTS, q * QW:(q + 1) * QW]
                dve.max(cand[:, q, :], part).then_inc(cand_set, 1)
                wait_apart(cand_set, t * NQ + (q + 1))
                dve.max_index(cidx[:, q, :], cand[:, q, :], part).then_inc(cidx_set, 1)

            def scan_row(t):
                cf = cand[:, :, :].rearrange("p q k -> p (q k)")
                gf = gidx[:, :, :].rearrange("p q k -> p (q k)")
                wait_apart(cand_set, t * NQ + NQ)
                dve.max(top8[:, :], cf).then_inc(top_set, 1)
                dve.wait_ge(cidx_set, t * NQ + NQ)
                dve.tensor_tensor(gf, cidx[:, :, :].rearrange("p q k -> p (q k)"),
                                  offs[:, :, :].rearrange("p q k -> p (q k)"), ALU.add).then_inc(gidx_set, 1)
                dve.wait_ge(top_set, t + 1)
                dve.wait_ge(gidx_set, t + 1)
                dve.scalar_tensor_tensor(out=gf, in0=cf, scalar=top8[:, 0:1], in1=gf, op0=ALU.is_equal,
                                         op1=ALU.mult, accum_out=pickf[:, :]).then_inc(pickf_set, 1)
                dve.tensor_copy(top2[:, bass.ds(t, 1), :].rearrange("p t k -> p (t k)"), top8[:, 0:2]
                                ).then_inc(scan_set, 1)
                dve.wait_ge(pickf_set, t + 1)
                dve.tensor_scalar(pick[:, bass.ds(t, 1)], pickf[:, :], float(N - 1), None, ALU.min
                                  ).then_inc(scan_set, 1)

            def logits(s, c, k):
                if k == 0:
                    dve.wait_ge(cidx_set, s * NQ + NQ)
                wait_apart(s_ready, s * NCH + (k + 1))
                part = ring[:, c % SLOTS, k * CH:(k + 1) * CH]
                dve.tensor_tensor_reduce(out=part, in0=S[(c * NCH + k) % 3][:, :], in1=part, scale=1.0,
                                         scalar=-3.0e38, op0=ALU.add, op1=ALU.max,
                                         accum_out=cmax[:, k:k + 1]).then_inc(s_used, 1)

            def step(s, c):
                score, value, follow = c < NT, 1 <= c <= NT, c >= 2
                if score:
                    logits(s, c, 0)
                if value:
                    dve.wait_ge(p_ready, s * NQ)
                    dve.tensor_reduce(rsum[:, :], sums[:, :], AX.X, ALU.add).then_inc(rsum_set, 1)
                if score:
                    logits(s, c, 1)
                if value:
                    dve.wait_ge(rsum_set, s)
                    if c >= 2:
                        dve.wait_ge(ctx_set, s - 1)
                    dve.reciprocal(rinv[:, :], rsum[:, :]).then_inc(rinv_set, 1)
                if follow:
                    dve.wait_ge(ctxT_hi, s - 1)
                    lo_part(postT[:, 1].rearrange("p c n -> p (c n)"), T[:, :], 1.0,
                            postT[:, 0].rearrange("p c n -> p (c n)")).then_inc(ctxT_lo, 1)
                if score:
                    logits(s, c, 2)
                    logits(s, c, 3)
                if follow:
                    dve.wait_ge(v_ready, s - 1)
                    dve.wait_ge(res_in, s * 16 - 16)
                    dve.scalar_tensor_tensor(out=res[:, :], in0=VF[:, :], scalar=1.0 / (W_UP * XV_UP), in1=res[:, :],
                                             op0=ALU.mult, op1=ALU.add).then_inc(h_set, 1)
                    dve.wait_ge(h_set, s - 1)
                    dve.bn_stats(stats[:, :], res[:, :]).then_inc(stats_set, 1)
                    wait_apart(stats_set, s - 1)
                    dve.bn_aggr(mv[:, :], stats[:, :]).then_inc(mv_set, 1)
                if score:
                    logits(s, c, 4)
                if value:
                    exponentials_lo(s - 1, 0)
                if follow:
                    dve.wait_ge(rstd_set, s - 1)
                    dve.tensor_scalar(res[:, :], res[:, :], mv[:, 0:1], rstd[:, :], ALU.subtract, ALU.mult
                                      ).then_inc(x1_set, 1)
                if score:
                    logits(s, c, 5)
                if value:
                    exponentials_lo(s - 1, 1)
                if score:
                    logits(s, c, 6)
                if follow:
                    dve.wait_ge(x1T_hi, s - 1)
                    lo_part(postT[:, 1].rearrange("p c n -> p (c n)"), T[:, :], X1_UP,
                            postT[:, 0].rearrange("p c n -> p (c n)")).then_inc(x1T_lo, 1)
                if score:
                    logits(s, c, 7)
                    dve.wait_ge(s_used, (s + 1) * NCH)
                    dve.tensor_reduce(rmax[:, :], cmax[:, :], AX.X, ALU.max).then_inc(rmax_set, 1)
                    dve.wait_ge(rmax_set, s + 1)
                    if c >= 1:
                        dve.wait_ge(p_ready, s * NQ)
                    dve.tensor_scalar(shift[:, :], rmax[:, :], -2.0, P_LOG2 * LN2, ALU.mult, ALU.add
                                      ).then_inc(shift_set, 1)
                for g in range(2, NCH):
                    if value:
                        exponentials_lo(s - 1, g)
                    if c < NT - 1 and g - 2 < NQ:
                        scan(s + 1, c + 1, g - 2)
                    if c < NT - 1 and g - 2 == NQ:
                        scan_row(s + 1)

            def exponentials_lo(t, g):
                dve.wait_ge(pt_hi, t * NCH + (g + 1))
                dve.tensor_tensor(pT[:, g % 2, 1, :], PT[g % 2][:, :], pT[:, g % 2, 0, :], ALU.subtract
                                  ).then_inc(pt_lo, 1)

            def prove_single():
                t2 = top2[:, :, :].rearrange("p t k -> p (t k)")
                mask, mag = okw[:, 64:128], okw[:, 128:192]
                by_row = mask.rearrange("p (t k) -> p t k", k=2)
                need, gap = okw[:, 192:224], okw[:, 224:256]
                steps = [0]

                def then(ins):
                    steps[0] += 1
                    ins.then_inc(ok_chain, 1)
                    dve.wait_ge(ok_chain, steps[0])

                dve.wait_ge(scan_set, 2 * NT)
                then(dve.tensor_scalar(mask, t2, -1.0, 1.0, ALU.mult, ALU.add))
                then(dve.tensor_scalar(mask, mask, NEG_INF, None, ALU.mult))
                then(dve.scalar_tensor_tensor(out=mag, in0=mask, scalar=-1.0, in1=mask, op0=ALU.mult, op1=ALU.max))
                by_row_mag = mag.rearrange("p (t k) -> p t k", k=2)
                then(dve.tensor_tensor(need, by_row_mag[:, :, 0], by_row_mag[:, :, 1], ALU.add))
                then(dve.tensor_scalar(need, need, 2.0 ** -22, thr[:, :], ALU.mult, ALU.add))
                then(dve.tensor_tensor(gap, by_row[:, :, 0], by_row[:, :, 1], ALU.subtract))
                then(dve.tensor_tensor(gap, gap, need, ALU.is_ge))
                then(dve.tensor_reduce(okw[:, 0:1], gap, AX.X, ALU.add))

            def last_rstd(e):
                t = slice(e * JB, (e + 1) * JB)
                dve.wait_ge(e_sd, e + 1)
                dve.reciprocal(e_r[:, t], e_s[:, t]).then_inc(e_chain, 1)
                dve.wait_ge(e_chain, e * 5 + 1)
                dve.tensor_tensor(e_t[:, t], e_r[:, t], e_r[:, t], ALU.mult).then_inc(e_chain, 1)
                dve.wait_ge(e_chain, e * 5 + 2)
                dve.scalar_tensor_tensor(out=e_t[:, t], in0=e_mean[:, t, 1], scalar=EPS, in1=e_t[:, t], op0=ALU.add,
                                         op1=ALU.mult).then_inc(e_chain, 1)
                dve.wait_ge(e_chain, e * 5 + 3)
                dve.tensor_scalar(e_t[:, t], e_t[:, t], -0.5, 1.5, ALU.mult, ALU.add).then_inc(e_chain, 1)
                dve.wait_ge(e_chain, e * 5 + 4)
                dve.tensor_tensor(e_r[:, t], e_r[:, t], e_t[:, t], ALU.mult).then_inc(e_chain, 1)
                dve.wait_ge(e_chain, e * 5 + 5)
                dve.scalar_tensor_tensor(out=e_nm[:, t], in0=e_mean[:, t, 0], scalar=-1.0, in1=e_r[:, t],
                                         op0=ALU.mult, op1=ALU.mult).then_inc(e_rstd, 1)

            def last_norm():
                for e in range(NE):
                    tiles = range(e * JB, (e + 1) * JB)
                    dve.wait_ge(x1r_in[e], 16)
                    dve.wait_ge(got_in[e], 16 * JB)
                    for t in tiles:
                        dve.scalar_tensor_tensor(out=got[:, t, :], in0=got[:, t, :], scalar=0.0, in1=x1r[:, t, :],
                                                 op0=ALU.max, op1=ALU.add).then_inc(e_sum, 1)
                    for t in tiles:
                        dve.wait_ge(e_sum, t + 1)
                        dve.bn_stats(e_st[:, t, :], got[:, t, :]).then_inc(e_stats, 1)
                    for t in tiles:
                        dve.wait_ge(e_stats, t + 1)
                        dve.bn_aggr(e_mean[:, t, :], e_st[:, t, :]).then_inc(e_mv, 1)
                    if e >= 1:
                        last_rstd(e - 1)
                last_rstd(NE - 1)

            dve.wait_ge(const_set, 1)
            for q in range(NQ):
                scan(0, 0, q)
            scan_row(0)
            run_steps(dve, step, NT // 3 - 1)
            prove_single()
            last_norm()
            dve.wait_ge(count_ready, 1)
            dve.tensor_copy(flag[:, :], S[0][0:1, 0:1]).then_inc(flag_set, 1)

            def general():
                with dve.Fori(0, NT) as t:
                    dve.wait_ge(ge_ready, t + 2)
                    dve.tensor_copy(g_enT[:, bass.ds(t * P, P)], S[0][0:H, 0:P]).then_inc(ge_copied, 1)
                    dve.tensor_copy(g_es[:, bass.ds(t, 1), :].rearrange("p t h -> p (t h)"), S[1][:, 0:H]
                                    ).then_inc(ge_copied, 1)
                dve.wait_ge(gen_out, 16)
                dve.wait_ge(ge_copied, 2 * NT + 1)
                with dve.Fori(0, H) as h:
                    with dve.Fori(0, NT) as t:
                        n = h * NT + t
                        dve.wait_ge(ga_in, n * 16 + 16)
                        dve.tensor_scalar(g_adj, g_adj, -1.0, 1.0, ALU.mult, ALU.add).then_inc(g_mask, 1)
                        dve.tensor_copy(thr[:, :], g_es[:, bass.ds(t, 1), bass.ds(h, 1)]
                                        .rearrange("p t h -> p (t h)")).then_inc(g_mask, 1)
                        dve.wait_ge(g_mask, n * 3 + 2)
                        dve.tensor_scalar(g_adj, g_adj, NEG_INF, None, ALU.mult).then_inc(g_mask, 1)
                        dve.wait_ge(gnb_in, h * 16 + 16)
                        dve.wait_ge(g_tr, n * NCH + 1)
                        dve.tensor_scalar(g_z, g_nb, thr[:, :], None, ALU.add).then_inc(g_z_set, 1)
                        dve.wait_ge(g_z_set, n + 2)
                        dve.scalar_tensor_tensor(out=g_z, in0=g_z, scalar=0.2, in1=g_z, op0=ALU.mult, op1=ALU.max
                                                 ).then_inc(g_inv, 1)
                        dve.wait_ge(g_inv, n * 3 + 1)
                        wait_apart(g_mask, n * 3 + 3)
                        dve.tensor_tensor_reduce(out=g_z, in0=g_z, in1=g_adj, scale=1.0, scalar=-3.0e38, op0=ALU.add,
                                                 op1=ALU.max, accum_out=rmax[:, :]).then_inc(g_log, 1)
                        dve.wait_ge(g_log, n + 2)
                        dve.tensor_scalar(shift[:, :], rmax[:, :], -1.0, None, ALU.mult).then_inc(g_shift, 1)
                        dve.wait_ge(g_exp, n + 1)
                        dve.reciprocal(rinv[:, :], rsum[:, :]).then_inc(g_inv, 1)
                        dve.wait_ge(g_inv, n * 3 + 2)
                        dve.wait_ge(g_mm, n * NCH + NCH + 1)
                        dve.tensor_scalar(g_row, O[:, 0:DH], rinv[:, :], None, ALU.mult).then_inc(g_inv, 1)
                        dve.wait_ge(g_inv, n * 3 + 3)
                        dve.tensor_copy(g_out[:, bass.ds(t, 1), bass.ds(h * DH, DH)].rearrange("p t d -> p (t d)"),
                                        g_row).then_inc(g_o, 1)
                dve.wait_ge(g_o, H * NT + 1)
                with dve.Fori(0, NT) as t:
                    dve.wait_ge(gx_in, t * 16 + 16 * (NT + 1))
                    dve.scalar_tensor_tensor(out=res[:, :], in0=g_out[:, bass.ds(t, 1), :].rearrange("p t d -> p (t d)"),
                                             scalar=0.0, in1=res[:, :], op0=ALU.max, op1=ALU.add).then_inc(gh_set, 1)
                    dve.wait_ge(gh_set, t + 1)
                    dve.bn_stats(stats[:, :], res[:, :]).then_inc(gh_stats, 1)
                    wait_apart(gh_stats, t + 1)
                    dve.bn_aggr(mv[:, :], stats[:, :]).then_inc(gh_mv, 1)
                    dve.wait_ge(gh_rstd, t + 1)
                    dve.tensor_scalar(res[:, :], res[:, :], mv[:, 0:1], rstd[:, :], ALU.subtract, ALU.mult
                                      ).then_inc(gh_fin, 1)

            if_general(dve, general, (ge_copied, g_z_set, g_log, g_o))


_INS = ["x", "adj", "L0_gnn_Wq", "L0_gnn_bq", "L0_gnn_Wk", "L0_gnn_Wv", "L0_gnn_bv", "L1_gnn_W", "L1_gnn_b",
        "L1_gnn_a_self", "L1_gnn_a_neigh"]


def kernel(**inputs):
    import numpy as np
    import concourse.bacc as bacc
    from concourse.bass_utils import run_bass_kernel_spmd

    nc = bacc.Bacc("TRN2", target_bir_lowering=False, num_devices=1)
    arrays, args = {}, []
    for name in _INS:
        a = np.ascontiguousarray(inputs[name])
        arrays[f"in_{name}"] = a
        args.append(nc.dram_tensor(f"in_{name}", a.shape, mybir.dt.from_np(a.dtype), kind="ExternalInput").ap())
    out = nc.dram_tensor("out", inputs["x"].shape, F32, kind="ExternalOutput").ap()
    adj_resnorm_kernel(nc, *args, out)
    r = run_bass_kernel_spmd(nc, [arrays], core_ids=[0])
    return r.results[0]["out"]
```

```python
from contextlib import ExitStack

import concourse.bass as bass
from concourse import mybir

ALU = mybir.AluOpType
ACT = mybir.ActivationFunctionType
AX = mybir.AxisListType
F32 = mybir.dt.float32
F16 = mybir.dt.float16
U32 = mybir.dt.uint32

P = 128
LN2 = 0.6931471805599453


def adj_resnorm_kernel(nc, x, adj, wq, bq, wk, wv, bv, w1, b1, a_self, a_neigh, out):
    N, D = x.shape
    H, _, DH = w1.shape
    NT = N // P
    KC = D // P
    CH = 512
    NCH = N // CH
    JB = CH // P
    NG = NT // JB
    NQ = 4
    QW = N // NQ
    SLOTS = 3
    assert D == 512 and N % CH == 0 and H * DH == D and NT % 3 == 2 and NG % 2 == 0

    W_UP = 32.0
    XT_UP = 0.125
    Y_UP = 8.0
    XV_UP = 32.0
    X1_UP = 8.0
    B_UP = 16.0
    P_LOG2 = 14
    HALF_SCALE = 0.5 / float(D) ** 0.5
    NEG_INF = -1.0e10
    EPS = 1.0e-5

    ctx = ExitStack()
    with ctx:
        def sb(name, shape, dt):
            return ctx.enter_context(nc.sbuf_tensor(name, shape, dt))

        def sem(name):
            return ctx.enter_context(nc.semaphore(name))

        def dram(name, shape, dt):
            return nc.dram_tensor(name, shape, dt, kind="Internal").ap()

        xT = sb("xT", [P, 2, KC, N], F16)
        xv = sb("xv", [P, 2, NT, D], F16)
        ring = sb("ring", [P, SLOTS, N], F32)
        wvT = sb("wvT", [P, 2, KC, D], F16)
        w1s = sb("w1s", [P, 2, KC, D], F16)
        yq = sb("yq", [P, 2, KC, P], F16)
        eT = sb("eT", [P, QW], F32)
        post = sb("post", [P, D], F32)
        res = sb("res", [P, D], F32)
        postT = sb("postT", [P, 2, KC, P], F16)
        brow = sb("brow", [P, D], F16)
        sel_v = sb("sel_v", [P, P], F16)
        sel_b = sb("sel_b", [P, P], F16)
        ident = sb("ident", [P, P], F32)
        top2 = sb("top2", [P, NT, 2], F32)
        pick = sb("pick", [P, NT], U32)
        cand = sb("cand", [P, NQ, 8], F32)
        cidx = sb("cidx", [P, NQ, 8], U32)
        gidx = sb("gidx", [P, NQ, 8], F32)
        offs = sb("offs", [P, NQ, 8], F32)
        top8 = sb("top8", [P, 8], F32)
        pickf = sb("pickf", [P, 1], F32)
        u = sb("u", [P, KC, 2 * H], F32)
        c8 = sb("c8", [P, KC], F32)
        bqc = sb("bqc", [P, KC], F32)
        bq16 = sb("bq16", [P, KC, 2], F16)
        csum = sb("csum", [P, KC], F32)
        usum = sb("usum", [P, 1], F32)
        ones = sb("ones", [P, 1], F32)
        eps = sb("eps", [P, 1], F32)
        mhalf = sb("mhalf", [P, 1], F32)
        thr = sb("thr", [P, 1], F32)
        cmax = sb("cmax", [P, NCH], F32)
        rmax = sb("rmax", [P, 1], F32)
        shift = sb("shift", [P, 1], F32)
        sums = sb("sums", [P, NQ], F32)
        rsum = sb("rsum", [P, 1], F32)
        rinv = sb("rinv", [P, 1], F32)
        stats = sb("stats", [P, 6], F32)
        mv = sb("mv", [P, 2], F32)
        ve = sb("ve", [P, 1], F32)
        rstd = sb("rstd", [P, 1], F32)
        flag = sb("flag", [1, 1], U32)

        pT = ring[:, :, :].bitcast(F16).rearrange("p s (q a n) -> p s q a n", q=NQ, a=2)

        wf = ring[:, 0, :].rearrange("p (a c n) -> p a c n", a=2, c=KC)
        m16 = ring[:, 1, 0:N // 2].bitcast(F16).rearrange("p (a c n) -> p a c n", a=2, c=KC)
        xs = [ring[:, 1, N // 2:N].rearrange("p (j n) -> p j n", j=JB),
              ring[:, 2, 0:N // 2].rearrange("p (j n) -> p j n", j=JB)]
        w16 = ring[:, 2, :].bitcast(F16).rearrange("p (w a c n) -> p w a c n", w=2, a=2, c=KC)
        ybuf = ring[:, 2, N // 2:N].bitcast(F16).rearrange("p (j a c n) -> p j a c n", j=JB, a=2, c=KC)
        wvf = xv[:, 0, 24:32, :].bitcast(F32).rearrange("p (c b) n -> p c (b n)", c=KC)
        w1f = xv[:, 1, 24:32, :].bitcast(F32).rearrange("p (c b) n -> p c (b n)", c=KC)
        prod = [xv[:, a, 16:24, :].bitcast(F32).rearrange("p (c b) n -> p c (b n)", c=KC) for a in range(2)]
        ab = [eT[:, s * D:(s + 1) * D] for s in range(2)]
        yf = [res, post]
        usq = top2[:, :, :].rearrange("p t k -> p (t k)")[:, 0:KC * 2 * H]
        brf = yq[:, :, :, :].bitcast(F32).rearrange("p a c n -> p (a c n)")
        brh = postT[:, 0, :, :].rearrange("p c n -> p (c n)")
        brl = postT[:, 1, :, :].rearrange("p c n -> p (c n)")

        S = [ctx.enter_context(nc.psum_tensor(f"S{k}", [P, CH], F32)) for k in range(3)]
        pt_banks = ctx.enter_context(nc.psum_tensor("PT", [P, 2 * CH], F32))
        PT = [pt_banks[:, 0:CH], pt_banks[:, CH:2 * CH]]
        O = ctx.enter_context(nc.psum_tensor("O", [P, CH], F32))
        T = ctx.enter_context(nc.psum_tensor("T", [P, CH], F32))
        VF = ctx.enter_context(nc.psum_tensor("VF", [P, CH], F32))

        ET = [eT, pt_banks]

        y_d = dram("y_scratch", [N, 2 * KC * P], F16)
        x1_d = dram("x1_scratch", [N, D], F32)
        f_d = dram("feats_scratch", [N, D], F32)

        wqk_in = [sem(f"wqk_in{o}") for o in range(KC)]
        bq_in, bq_hi, bq_lo, csum_set = map(sem, ("bq_in", "bq_hi", "bq_lo", "csum_set"))
        wv_in, w1_in, small_in, a_in = map(sem, ("wv_in", "w1_in", "small_in", "a_in"))
        xs_in = [sem("xs_in0"), sem("xs_in1")]
        const_set, brf_zero = sem("const_set"), sem("brf_zero")
        sel_set = sem("sel_set")
        ident_zero, ident_set = sem("ident_zero"), sem("ident_set")
        w_hi, w_lo = sem("w_hi"), sem("w_lo")
        m_ready, m_hi, m_lo = sem("m_ready"), sem("m_hi"), sem("m_lo")
        c_ready, c_set = sem("c_ready"), sem("c_set")
        wvT_ready, wvT_hi, wvT_lo = sem("wvT_ready"), sem("wvT_hi"), sem("wvT_lo")
        w1_hi, w1_lo = sem("w1_hi"), sem("w1_lo")
        br_hi, br_lo, br_set = sem("br_hi"), sem("br_lo"), sem("br_set")
        prod_set, u_set, usq_set, usum_ready, thr_set = map(sem, ("prod_set", "u_set", "usq_set", "usum_ready", "thr_set"))
        onesq_set = sem("onesq_set")
        xt_ready, xt_hi, xt_lo = sem("xt_ready"), sem("xt_hi"), sem("xt_lo")
        yp_ready, y_f, y_hi, y_lo = sem("yp_ready"), sem("y_f"), sem("y_hi"), sem("y_lo")
        xv_hi, xv_lo = sem("xv_hi"), sem("xv_lo")
        y_out = sem("y_out")
        adj_in = sem("adj_in")
        y_in, res_in, x1_out, f_out = map(sem, ("y_in", "res_in", "x1_out", "f_out"))
        s_ready, s_used = sem("s_ready"), sem("s_used")
        rmax_set, shift_set = sem("rmax_set"), sem("shift_set")
        p_ready, rsum_set, rinv_set = sem("p_ready"), sem("rsum_set"), sem("rinv_set")
        pt_ready, pt_hi, pv_done = sem("pt_ready"), sem("pt_hi"), sem("pv_done")
        pt_lo = [sem("pt_lo_even"), sem("pt_lo_odd")]
        ctx_set, ctxT_ready, ctxT_hi, ctxT_lo = map(sem, ("ctx_set", "ctxT_ready", "ctxT_hi", "ctxT_lo"))
        v_ready, h_set, stats_set, mv_set, ve_set, rstd_set = map(
            sem, ("v_ready", "h_set", "stats_set", "mv_set", "ve_set", "rstd_set"))
        x1_set, x1T_ready, x1T_hi, x1T_lo = map(sem, ("x1_set", "x1T_ready", "x1T_hi", "x1T_lo"))
        f_ready, f_set = sem("f_ready"), sem("f_set")
        cand_set, cidx_set = sem("cand_set"), sem("cidx_set")
        top_set, gidx_set, pickf_set, scan_set = map(sem, ("top_set", "gidx_set", "pickf_set", "scan_set"))
        ok_chain, count_ready, flag_set = sem("ok_chain"), sem("count_ready"), sem("flag_set")
        NE = NT // JB
        e_neg, e_square = sem("e_neg"), sem("e_square")
        x1r_in = [sem(f"x1r_in{e}") for e in range(NE)]
        got_in = [sem(f"got_in{e}") for e in range(NE)]
        e_sum, e_stats, e_mv, e_sd, e_chain, e_rstd, e_out, out_done = map(
            sem, ("e_sum", "e_stats", "e_mv", "e_sd", "e_chain", "e_rstd", "e_out", "out_done"))

        x1r = xT[:, :, :, :].bitcast(F32).rearrange("p a c n -> p (a c n)").rearrange("p (t d) -> p t d", d=D)
        got = xv[:, :, :, :].bitcast(F32).rearrange("p a t n -> p (a t n)").rearrange("p (t d) -> p t d", d=D)
        end = ring[:, 2, :]
        e_st = end[:, 0:NT * 6].rearrange("p (t s) -> p t s", s=6)
        e_mean = end[:, 256:256 + 2 * NT].rearrange("p (t s) -> p t s", s=2)
        e_s = end[:, 384:384 + NT]
        e_r = end[:, 448:448 + NT]
        e_t = end[:, 512:512 + NT]
        e_nm = end[:, 576:576 + NT]
        okw = ring[:, 2, 1024:1024 + 8 * NT]
        onesq = x1r[:, NT - 1, 0:P]
        e_tot = ring[:, 2, 640:640 + NT]
        e_junk = ring[:, 0:2, :].rearrange("p s n -> p (s n)").rearrange("p (t d) -> p t d", d=D)

        g_adj, g_z, g_nb = ring[:, 0, :], ring[:, 1, :], ring[:, 2, :]
        g_feats, g_out = x1r, got
        g_p = [wvT[:, a, :, :].bitcast(F32).rearrange("p c n -> p (c n)")[:, 0:CH] for a in range(2)]
        g_xT = w1s[:, 0, :, :].bitcast(F32).rearrange("p c n -> p (c n)")[:, 0:D]
        g_es = w1s[:, 1, :, :].bitcast(F32).rearrange("p c n -> p (c n)")[:, 0:NT * H]\
            .rearrange("p (t h) -> p t h", h=H)
        g_enT = ring[0:H, 0, :]
        g_row = brow[:, 0:2 * DH].bitcast(F32)
        en_d = dram("e_neigh_scratch", [H, N], F32)
        (gx_in, gT_ready, gT_copied, ge_ready, ge_copied, gen_out, gf_in, gnb_in, ga_in, g_mask, g_log, g_z_set,
         g_shift, g_exp, g_tr, g_pc, g_mm, g_o, g_inv, gh_set, gh_stats, gh_mv, gh_ve, gh_rstd, gh_fin, gh_out
         ) = (sem(f"general_{name}") for name in (
             "x1_in", "x1T_ready", "x1T_copied", "e_ready", "e_copied", "e_neigh_out", "feats_in", "neigh_in",
             "adj_in", "mask", "logits", "z", "shift", "exp", "transposed", "p_copied", "multiplied", "out_set",
             "inv", "h", "stats", "mv", "ve", "rstd", "final", "out"))

        def if_general(eng, path, from_one=()):
            eng.wait_ge(flag_set, 1)
            with eng.register("proven") as proven:
                eng.reg_load(proven, flag[0:1, 0:1])
                with eng.If_ne(proven, N):
                    eng.wait_ge(out_done, 16 * (NE + 1))
                    for semaphore in from_one:
                        eng.sem_inc(semaphore, 1)
                    path()

        block = ctx.enter_context(nc.Block())

        def run_steps(eng, step, rounds, first=2):
            for s in range(first):
                step(s, s)
            with eng.Fori(0, rounds) as i:
                for k in range(3):
                    step(i * 3 + (first + k), first + k)
            for s in range(first + 3 * rounds, NT + 2):
                step(s, s)

        def run_groups(eng, transposed, queries, between):
            transposed(0, 0)
            queries(0, 0, range(0, 1))
            between(0)
            queries(0, 0, range(1, KC - 1))
            transposed(1, 1)
            queries(0, 0, range(KC - 1, KC))
            between(1)
            for g in (2, 3):
                transposed(g, g)
                queries(g - 1, g - 1, range(KC))
                between(g)
            with eng.Fori(1, NG // 2 - 1) as i:
                for k in range(2):
                    transposed(i * 2 + (k + 2), k + 4)
                    queries(i * 2 + (k + 1), k + 3, range(KC))
            between(4)
            queries(NG - 1, NG - 1, range(KC))
            between(5)

        @block.sync
        def _(sp):
            yq_flat = yq[:, :, :, :].rearrange("p a c n -> p (a c n)")
            for o in range(KC):
                for w, weights in enumerate((wq, wk)):
                    sp.dma_start(wf[:, w, o, :], weights[o * P:(o + 1) * P, :]).then_inc(wqk_in[o], 16)
            sp.dma_start(bqc[:, :], bq.rearrange("(c p) -> p c", p=P), allow_slow_non_contiguous=True).then_inc(bq_in, 16)

            def load_x(g, k):
                sp.dma_start(xs[k % 2], x[bass.ds(g * (JB * P), JB * P), :]
                             .rearrange("(j p) n -> p j n", p=P)).then_inc(xs_in[k % 2], 16)

            load_x(0, 0)
            sp.dma_start(wvf, wv.rearrange("(c p) n -> p c n", p=P)).then_inc(wv_in, 16)
            sp.wait_ge(brf_zero, 1)
            b1_row = b1.rearrange("h d -> (h d)").rearrange("(a n) -> a n", a=1)
            bv_row = bv.rearrange("(a n) -> a n", a=1)
            for row, vec in ((0, bv_row), (32, bv_row), (64, b1_row), (96, b1_row)):
                sp.dma_start(brf[row:row + 1, :], vec).then_inc(small_in, 16)
            for k, a in enumerate((a_self, a_neigh)):
                sp.dma_start(ab[k], a.rearrange("h d -> (h d)").rearrange("(a n) -> a n", a=1)
                             .broadcast_to([P, D])).then_inc(a_in, 16)
            for kc in range(KC):
                sp.dma_start(w1f[:, kc, :].rearrange("p (h d) -> p h d", h=H),
                             w1[:, kc * P:(kc + 1) * P, :].rearrange("h p d -> p h d")).then_inc(w1_in, 16)
            sp.wait_ge(m_ready, KC)
            load_x(1, 1)

            def store_queries(g):
                sp.wait_ge(y_lo, (g + 1) * KC)
                sp.dma_start(y_d[bass.ds(g * (JB * P), JB * P), :].rearrange("(j p) m -> p j m", p=P),
                             ybuf.rearrange("p j a c n -> p j (a c n)")).then_inc(y_out, 16)

            def group(g, k):
                sp.wait_ge(xt_ready, (g + 1) * KC)
                sp.wait_ge(xv_hi, g + 1)
                sp.wait_ge(xv_lo, g + 1)
                load_x(g + 2, k)
                store_queries(g)

            group(0, 0)
            group(1, 1)
            with sp.Fori(1, NG // 2 - 1) as i:
                for k in range(2):
                    group(i * 2 + k, k)
            sp.wait_ge(w_lo, KC)
            sp.dma_start(ring[:, 0, :], adj[0:P, :]).then_inc(adj_in, 16)
            sp.wait_ge(y_out, 16)
            sp.wait_ge(br_set, 1)
            sp.dma_start(yq_flat, y_d[0:P, :]).then_inc(y_in, 16)
            sp.wait_ge(y_in, 16)
            sp.dma_start(postT[:, :, :, :].rearrange("p a c n -> p (a c n)"), y_d[P:2 * P, :]).then_inc(y_in, 16)
            store_queries(NG - 2)
            store_queries(NG - 1)
            sp.wait_ge(y_out, 16 * NG)
            sp.wait_ge(yp_ready, KC * NG)
            sp.wait_ge(xv_hi, NG)
            sp.wait_ge(xv_lo, NG)
            sp.wait_ge(adj_in, 16)
            sp.dma_start(ring[:, 1, :], adj[P:2 * P, :]).then_inc(adj_in, 16)

            def step(s, c):
                if c == NT:
                    sp.wait_ge(s_ready, NT * NCH)
                    sp.wait_ge(x1_out, 16 * (NT - 2))
                    for e in range(NE - 1):
                        load_x1(e, e * JB, (e + 1) * JB)
                if 1 <= c < NT - 1:
                    if c >= 2:
                        sp.wait_ge(pv_done, s - 1)
                    sp.wait_ge(adj_in, s * 16 + 16)
                    sp.dma_start(ring[:, (c + 1) % SLOTS, :], adj[bass.ds((s + 1) * P, P), :]
                                 ).then_inc(adj_in, 16)
                if c >= 2:
                    sp.wait_ge(x1_set, s - 1)
                    sp.dma_start(x1_d[bass.ds((s - 2) * P, P), :], res[:, :]).then_inc(x1_out, 16)
                if c < NT - 1 and c != 1:
                    sp.wait_ge(s_ready, (s + 1) * NCH)
                    sp.dma_start(yq_flat, y_d[bass.ds((s + 1 + (c == 0)) * P, P), :]).then_inc(y_in, 16)
                if 1 <= c <= NT:
                    if c >= 2:
                        sp.wait_ge(x1_out, (s - 1) * 16)
                        sp.wait_ge(x1T_ready, s - 1)
                    else:
                        sp.wait_ge(y_lo, KC * NG)
                    sp.dma_start(res[:, :], x[bass.ds((s - 1) * P, P), :]).then_inc(res_in, 16)
                if c >= 2:
                    sp.wait_ge(f_set, s - 1)
                    sp.dma_start(f_d[bass.ds((s - 2) * P, P), :], post[:, :]).then_inc(f_out, 16)
                if c == NT:
                    sp.wait_ge(x1_out, 16 * (NT - 1))
                    load_x1(NE - 1, NT - JB, NT - 1)

            def load_x1(e, first, end):
                sp.dma_start(x1r[:, first:end, :], x1_d[first * P:end * P, :].rearrange("(j p) n -> p j n", p=P)
                             ).then_inc(x1r_in[e], 16)

            run_steps(sp, step, NT // 3 - 1)
            sp.wait_ge(x1_out, 16 * NT)
            load_x1(NE - 1, NT - 1, NT)
            ends = [(e + 1) * JB for e in range(NE - 1)] + [NT - JB // 2, NT]
            for first, end in zip([0] + ends, ends):
                sp.wait_ge(e_out, end)
                sp.dma_start(out[first * P:end * P, :].rearrange("(j p) n -> p j n", p=P),
                             got[:, first:end, :]).then_inc(out_done, 16)
            sp.wait_ge(out_done, 16 * (NE + 1))
            sp.wait_ge(f_out, 16 * NT)

            def general():
                with sp.Fori(0, NT) as t:
                    sp.wait_ge(gT_ready, t + 1)
                    sp.dma_start(res[:, :], x1_d[bass.ds(t * P, P), :]).then_inc(gx_in, 16)
                sp.dma_start(g_feats, f_d.rearrange("(t p) n -> p t n", p=P)).then_inc(gf_in, 16)
                sp.wait_ge(ge_copied, 2 * NT + 1)
                sp.dma_start(en_d, g_enT).then_inc(gen_out, 16)
                sp.wait_ge(gen_out, 16)
                with sp.Fori(0, H) as h:
                    sp.wait_ge(g_z_set, h * NT + 1)
                    sp.dma_start(g_nb, en_d[bass.ds(h, 1), :].broadcast_to([P, N])).then_inc(gnb_in, 16)
                    with sp.Fori(0, NT) as t:
                        sp.wait_ge(g_log, h * NT + t + 1)
                        sp.dma_start(g_adj, adj[bass.ds(t * P, P), :]).then_inc(ga_in, 16)
                sp.dma_start(res[:, :], x1_d[0:P, :]).then_inc(gx_in, 16)
                with sp.Fori(0, NT - 1) as t:
                    sp.wait_ge(gh_fin, t + 1)
                    sp.dma_start(out[bass.ds(t * P, P), :], res[:, :]).then_inc(gh_out, 16)
                    sp.wait_ge(gh_out, t * 16 + 16)
                    sp.dma_start(res[:, :], x1_d[bass.ds((t + 1) * P, P), :]).then_inc(gx_in, 16)
                sp.wait_ge(gh_fin, NT)
                sp.dma_start(out[N - P:N, :], res[:, :]).then_inc(gh_out, 16)
                sp.wait_ge(gh_out, 16 * NT)

            if_general(sp, general)

        @block.gpsimd
        def _(pool):
            pool.memset(brf[:, :], 0.0).then_inc(brf_zero, 1)
            pool.memset(ident[:, :], 0.0).then_inc(ident_zero, 1)
            pool.wait_ge(ident_zero, 1)
            pool.affine_select(out=ident[:, :], in_=ident[:, :], compare_op=ALU.not_equal, fill=1.0,
                               base=0, pattern=[[-1, P]], channel_multiplier=1).then_inc(ident_set, 1)
            pool.memset(ones[:, :], 1.0)
            pool.memset(eps[:, :], EPS)
            pool.memset(mhalf[:, :], -0.5)
            for q in range(NQ):
                last = pool.memset(offs[:, q, :], float(q * QW))
            last.then_inc(const_set, 1)
            pool.wait_ge(w1_in, 16 * KC)
            pool.wait_ge(a_in, 32)
            for k in range(2):
                for kc in range(KC):
                    pool.tensor_tensor(prod[k][:, kc, :], w1f[:, kc, :], ab[k], ALU.mult).then_inc(prod_set, 1)

            def exponentials_lo(t, c, q):
                pool.wait_ge(pt_hi, t * NQ + (q + 1))
                pool.tensor_tensor(pT[:, c % SLOTS, q, 1, :], eT[:, :], pT[:, c % SLOTS, q, 0, :], ALU.subtract
                                   ).then_inc(pt_lo[0], 1)

            def step(s, c):
                score, value, follow = c < NT, 1 <= c <= NT, c >= 2
                if follow:
                    pool.wait_ge(mv_set, s - 1)
                    pool.tensor_tensor(ve[:, :], mv[:, 1:2], eps[:, :], ALU.add).then_inc(ve_set, 1)
                    pool.wait_ge(ve_set, s - 1)
                    pool.tensor_tensor(rstd[:, :], ve[:, :], mhalf[:, :], ALU.pow).then_inc(rstd_set, 1)
                if c == NT:
                    pool.wait_ge(s_ready, NT * NCH)
                    pool.memset(onesq, 1.0).then_inc(onesq_set, 1)
                if score:
                    for q in range(0, NQ, 2):
                        exponentials_lo(s, c, q)

            run_steps(pool, step, NT // 3)

            pool.wait_ge(f_out, 16 * NT)
            pool.wait_ge(scan_set, 2 * NT)
            for t in range(NT):
                pool.indirect_dma_start(out=got[:, t, :], out_offset=None, in_=f_d,
                                        in_offset=bass.IndirectOffsetOnAxis(ap=pick[:, t:t + 1], axis=0)
                                        ).then_inc(got_in[t // JB], 16)

            def general():
                with pool.Fori(0, NT) as t:
                    pool.wait_ge(gh_mv, t + 1)
                    pool.tensor_tensor(ve[:, :], mv[:, 1:2], eps[:, :], ALU.add).then_inc(gh_ve, 1)
                    pool.wait_ge(gh_ve, t + 1)
                    pool.tensor_tensor(rstd[:, :], ve[:, :], mhalf[:, :], ALU.pow).then_inc(gh_rstd, 1)

            if_general(pool, general)

        @block.tensor
        def _(pe):
            Y = [S[0], S[1], S[2], VF]
            X = [PT[0], PT[1], O, T]

            def split_product(psum, sta, mov, n, first=True, last=True):
                for k in range(n):
                    for a, b in ((0, 0), (0, 1), (1, 0)):
                        mm = pe.matmul(psum, sta(a, k), mov(b, k), start=(first and k == 0 and a + b == 0),
                                       stop=(last and k == n - 1 and a == 1))
                return mm

            for o in range(KC):
                pe.wait_ge(w_lo, o + 1)
                for ic in range(KC):
                    for a, b in ((0, 0), (0, 1), (1, 0)):
                        mm = pe.matmul(Y[ic][:, :], w16[:, 0, a, o, ic * P:(ic + 1) * P], w16[:, 1, b, o, :],
                                       start=(o + a + b == 0), stop=(o == KC - 1 and a == 1))
                    if o == KC - 1:
                        mm.then_inc(m_ready, 1)
            pe.wait_ge(bq_lo, 1)
            for jc in range(KC):
                for o in range(KC):
                    for a in range(2):
                        mm = pe.matmul(T[:, 2 * jc:2 * jc + 2], w16[:, 1, a, o, jc * P:(jc + 1) * P], bq16[:, o, :],
                                       start=(o + a == 0), stop=(o == KC - 1 and a == 1))
            mm.then_inc(c_ready, 1)
            pe.wait_ge(ident_set, 1)

            def transposed(g, c):
                pe.wait_ge(xs_in[c % 2], (g - c % 2) * 8 + 16)
                for kc in range(KC):
                    if c >= 1:
                        pe.wait_ge(xt_lo, g * KC + (kc + 1 - KC))
                    if c == 1:
                        pe.wait_ge(wvT_lo, kc + 1)
                    if c == 0 and kc == KC - 1:
                        pe.wait_ge(csum_set, 1)
                    for j in range(JB):
                        mm = pe.transpose(X[kc][:, j * P:(j + 1) * P], xs[c % 2][:, j, kc * P:(kc + 1) * P],
                                          ident[:, :])
                    mm.then_inc(xt_ready, 1)

            def queries(g, c, jcs):
                pe.wait_ge(xt_lo, g * KC + KC)
                if c == 0:
                    pe.wait_ge(m_lo, KC)
                for jc in jcs:
                    if c >= 1:
                        pe.wait_ge(y_hi, g * KC + (jc + 1 - KC))
                    split_product(Y[jc][:, :], lambda a, k: m16[:, a, k, jc * P:(jc + 1) * P],
                                  lambda b, k: xT[:, b, k, bass.ds(g * CH, CH)], KC).then_inc(yp_ready, 1)

            def between(n):
                if n == 0:
                    pe.wait_ge(wv_in, 16)
                    for ic in range(KC):
                        for o in range(KC):
                            mm = pe.transpose(X[ic][:, o * P:(o + 1) * P], wvf[:, o, ic * P:(ic + 1) * P], ident[:, :])
                        mm.then_inc(wvT_ready, 1)

            run_groups(pe, transposed, queries, between)

            def scores(s, c, k):
                if k == 0:
                    pe.wait_ge(y_in, s * 16 + 16)
                    if c == 0:
                        pe.wait_ge(y_hi, KC * NG)
                n = c * NCH + k
                if n >= 3:
                    pe.wait_ge(s_used, s * NCH + (k - 2))
                tile_queries = postT if c == 1 else yq
                split_product(S[n % 3][:, :], lambda a, kc: tile_queries[:, a, kc, :],
                              lambda b, kc: xT[:, b, kc, k * CH:(k + 1) * CH], KC).then_inc(s_ready, 1)

            def values(t, c, g):
                q = g // 2
                pe.wait_ge(pt_lo[q % 2], t * (NQ // 2) + (q // 2 + 1))
                if g == 0 and c >= 1:
                    pe.wait_ge(ctx_set, t)
                first = (g % 2) * CH
                mm = split_product(O[:, :], lambda a, j: pT[:, c % SLOTS, q, a, first + j * P:first + (j + 1) * P],
                                   lambda b, j: xv[:, b, g * JB + j, :], JB, g == 0, g == NCH - 1)
                if g == NCH - 1:
                    mm.then_inc(pv_done, 1)

            def transpose_ctx(t):
                pe.wait_ge(ctx_set, t + 1)
                for kc in range(KC):
                    mm = pe.transpose(T[:, kc * P:(kc + 1) * P], post[:, kc * P:(kc + 1) * P], ident[:, :])
                mm.then_inc(ctxT_ready, 1)

            def project_values(t, c):
                pe.wait_ge(ctxT_lo, t + 1)
                if c >= 1:
                    pe.wait_ge(f_set, t)
                pe.matmul(VF[:, :], sel_v[:, :], brow[:, :], start=True, stop=False)
                split_product(VF[:, :], lambda a, k: postT[:, a, k, :], lambda b, k: wvT[:, b, k, :], KC, False
                              ).then_inc(v_ready, 1)

            def transpose_x1(t):
                pe.wait_ge(x1_set, t + 1)
                for kc in range(KC):
                    mm = pe.transpose(T[:, kc * P:(kc + 1) * P], res[:, kc * P:(kc + 1) * P], ident[:, :])
                mm.then_inc(x1T_ready, 1)

            def feats(t):
                pe.wait_ge(x1T_lo, t + 1)
                pe.matmul(VF[:, :], sel_b[:, :], brow[:, :], start=True, stop=False)
                split_product(VF[:, :], lambda a, k: postT[:, a, k, :], lambda b, k: w1s[:, b, k, :], KC, False
                              ).then_inc(f_ready, 1)

            def step(s, c):
                score, value, follow = c < NT, 1 <= c <= NT, c >= 2
                for k in range(NCH):
                    if score:
                        scores(s, c, k)
                    if c == NT:
                        values(s - 1, c - 1, k)
                        if k == 0:
                            transpose_ctx(s - 2)
                        if k == 2:
                            project_values(s - 2, c - 2)
                        if k == 5:
                            transpose_x1(s - 2)
                        if k == 6:
                            feats(s - 2)
                        continue
                    if follow and k == 1:
                        transpose_ctx(s - 2)
                    if follow and k == 3:
                        project_values(s - 2, c - 2)
                    if follow and k == 7:
                        transpose_x1(s - 2)
                for g in range(NCH):
                    if value and c < NT:
                        values(s - 1, c - 1, g)
                    if follow and c != NT and g == 1:
                        feats(s - 2)
                if c == NT:
                    pe.wait_ge(s_used, NT * NCH)
                    pe.wait_ge(onesq_set, 1)
                    pe.matmul(S[1][:, 0:1], onesq, usum[:, :], start=True, stop=True).then_inc(usum_ready, 1)

            pe.wait_ge(br_set, 1)
            pe.wait_ge(sel_set, 1)
            pe.wait_ge(w1_lo, 1)
            run_steps(pe, step, NT // 3)
            pe.wait_ge(ok_chain, 8)
            pe.matmul(S[0][0:1, 0:1], okw[:, 0:1], ones[:, :], start=True, stop=True).then_inc(count_ready, 1)

            def general():
                with pe.Fori(0, NT) as t:
                    pe.wait_ge(gx_in, t * 16 + 16)
                    pe.wait_ge(gT_copied, t + 1)
                    for kc in range(KC):
                        mm = pe.transpose(T[:, kc * P:(kc + 1) * P], res[:, kc * P:(kc + 1) * P], ident[:, :])
                    mm.then_inc(gT_ready, 1)
                    pe.wait_ge(gT_copied, t + 2)
                    pe.wait_ge(ge_copied, t * 2 + 1)
                    for kc in range(KC):
                        pe.matmul(S[0][0:H, 0:P], u[:, kc, H:2 * H], g_xT[:, kc * P:(kc + 1) * P],
                                  start=(kc == 0), stop=(kc == KC - 1))
                    for kc in range(KC):
                        mm = pe.matmul(S[1][:, 0:H], g_xT[:, kc * P:(kc + 1) * P], u[:, kc, 0:H],
                                       start=(kc == 0), stop=(kc == KC - 1))
                    mm.then_inc(ge_ready, 1)
                pe.wait_ge(gf_in, 16)
                with pe.Fori(0, H) as h:
                    with pe.Fori(0, NT) as t:
                        n = h * NT + t
                        pe.wait_ge(g_exp, n + 1)
                        for g in range(NCH):
                            pe.wait_ge(g_pc, n * NCH + max(g - 1, 0) + 1)
                            for j in range(JB):
                                m = (g * JB + j) * P
                                mm = pe.transpose(PT[g % 2][:, j * P:(j + 1) * P], g_z[:, m:m + P], ident[:, :])
                            mm.then_inc(g_tr, 1)
                            pe.wait_ge(g_pc, n * NCH + (g + 1) + 1)
                            if g == 0:
                                pe.wait_ge(g_o, n + 1)
                            for j in range(JB):
                                mm = pe.matmul(O[:, 0:DH], g_p[g % 2][:, j * P:(j + 1) * P],
                                               g_feats[:, g * JB + j, bass.ds(h * DH, DH)],
                                               start=(g == 0 and j == 0), stop=(g == NCH - 1 and j == JB - 1))
                            mm.then_inc(g_mm, 1)

            if_general(pe, general, (gT_ready, ge_ready, g_tr, g_mm))

        @block.scalar
        def _(act):
            Y = [S[0], S[1], S[2], VF]
            X = [PT[0], PT[1], O, T]

            def scaled(dst, src, scale):
                return nc.scalar.activation(dst, src, ACT.Copy, scale=scale)

            for o in range(KC):
                act.wait_ge(wqk_in[o], 32)
                scaled(w16[:, :, 0, o, :], wf[:, :, o, :], W_UP).then_inc(w_hi, 1)
            act.wait_ge(bq_in, 16)
            scaled(bq16[:, :, 0], bqc[:, :], B_UP).then_inc(bq_hi, 1)
            for ic in range(KC):
                act.wait_ge(m_ready, ic + 1)
                scaled(m16[:, 0, ic, :], Y[ic][:, :], 1.0 / W_UP).then_inc(m_hi, 1)

            def transposed(g, c):
                for kc in range(KC):
                    act.wait_ge(xt_ready, g * KC + (kc + 1))
                    scaled(xT[:, 0, kc, bass.ds(g * CH, CH)], X[kc][:, :], XT_UP).then_inc(xt_hi, 1)
                act.wait_ge(xs_in[c % 2], (g - c % 2) * 8 + 16)
                scaled(xv[:, 0, bass.ds(g * JB, JB), :], xs[c % 2], XV_UP).then_inc(xv_hi, 1)

            def queries(g, c, jcs):
                for jc in jcs:
                    act.wait_ge(yp_ready, g * KC + (jc + 1))
                    if c + jc == 0:
                        act.wait_ge(c_set, 1)
                    if c * KC + jc >= 2:
                        act.wait_ge(y_lo, g * KC + (jc - 1))
                    nc.scalar.activation(yf[jc % 2][:, :], Y[jc][:, :], ACT.Identity, bias=c8[:, jc:jc + 1],
                                         scale=HALF_SCALE * Y_UP / (W_UP * XT_UP)).then_inc(y_f, 1)
                    if jc == 0:
                        if c >= 1:
                            act.wait_ge(y_out, g * 16)
                        else:
                            act.wait_ge(c_ready, 1)
                    nc.scalar.activation(ybuf[:, :, 0, jc, :], Y[jc][:, :].rearrange("p (j n) -> p j n", j=JB),
                                         ACT.Identity, bias=c8[:, jc:jc + 1],
                                         scale=HALF_SCALE * Y_UP / (W_UP * XT_UP)).then_inc(y_hi, 1)

            def between(n):
                if n == 0:
                    for ic in range(KC):
                        act.wait_ge(wvT_ready, ic + 1)
                        scaled(wvT[:, 0, ic, :], X[ic][:, :], W_UP).then_inc(wvT_hi, 1)
                if n == 1:
                    act.wait_ge(w1_in, 16 * KC)
                    scaled(w1s[:, 0], w1f, W_UP).then_inc(w1_hi, 1)
                if n == 3:
                    act.wait_ge(w1_lo, 1)
                    act.wait_ge(u_set, 2)

            run_groups(act, transposed, queries, between)

            def exponentials(s, c, q):
                if q == 0:
                    act.wait_ge(shift_set, s + 1)
                    if c >= 1:
                        act.wait_ge(rsum_set, s)
                row = ring[:, c % SLOTS, q * QW:(q + 1) * QW]
                nc.scalar.activation(row, row, ACT.Exp, bias=shift[:, :], scale=2.0,
                                     accum_out=sums[:, q:q + 1]).then_inc(p_ready, 1)

            def exponentials_hi(t, c, q):
                act.wait_ge(pt_ready, t * NQ + (q + 1))
                scaled(pT[:, c % SLOTS, q, 0, :], ET[q % 2][:, :], 1.0).then_inc(pt_hi, 1)

            def step(s, c):
                score, value, follow = c < NT, 1 <= c <= NT, c >= 2
                if follow:
                    act.wait_ge(ctxT_ready, s - 1)
                    if c >= 3:
                        act.wait_ge(f_ready, s - 2)
                    scaled(postT[:, 0].rearrange("p c n -> p (c n)"), T[:, :], 1.0).then_inc(ctxT_hi, 1)
                if value:
                    exponentials_hi(s - 1, c - 1, NQ - 1)
                if follow:
                    act.wait_ge(x1T_ready, s - 1)
                    scaled(postT[:, 0].rearrange("p c n -> p (c n)"), T[:, :], X1_UP).then_inc(x1T_hi, 1)
                if score:
                    for q in range(NQ):
                        exponentials(s, c, q)
                    exponentials_hi(s, c, 0)
                if follow:
                    act.wait_ge(f_ready, s - 1)
                    scaled(post[:, :], VF[:, :], 1.0 / (W_UP * X1_UP)).then_inc(f_set, 1)
                if score:
                    for q in range(1, NQ - 1):
                        exponentials_hi(s, c, q)
                if value:
                    act.wait_ge(pv_done, s)
                    act.wait_ge(rinv_set, s)
                    if c >= 2:
                        act.wait_ge(f_out, s * 16 - 16)
                    nc.scalar.activation(post[:, :], O[:, :], ACT.Identity, scale=rinv[:, :]).then_inc(ctx_set, 1)

            run_steps(act, step, NT // 3)

            def normalise(e):
                act.wait_ge(e_rstd, e + 1)
                for t in range(e * JB, (e + 1) * JB):
                    nc.scalar.activation(got[:, t, :], got[:, t, :], ACT.Identity, bias=e_nm[:, t:t + 1],
                                         scale=e_r[:, t:t + 1]).then_inc(e_out, 1)

            for e in range(NE):
                tiles = slice(e * JB, (e + 1) * JB)
                if e % 2:
                    act.wait_ge(e_neg, e // 2 + 1)
                    for t in range(e * JB, (e + 1) * JB):
                        nc.scalar.activation(e_junk[:, t // (2 * JB) * JB + t % JB, :], got[:, t, :], ACT.Square,
                                             bias=e_mean[:, t, 0:1], accum_out=e_mean[:, t, 1:2]).then_inc(e_square, 1)
                    act.wait_ge(e_square, (e // 2 + 1) * JB)
                else:
                    act.wait_ge(e_mv, (e // 2 + 1) * JB)
                nc.scalar.activation(e_s[:, tiles], e_mean[:, tiles, 1], ACT.Sqrt, bias=eps[:, :],
                                     scale=1.0 / D if e % 2 else 1.0).then_inc(e_sd, 1)
                if e >= 1:
                    normalise(e - 1)
            normalise(NE - 1)

            def general():
                with act.Fori(0, NT) as t:
                    act.wait_ge(gT_ready, t + 2)
                    act.wait_ge(ge_ready, t + 1)
                    scaled(g_xT, T[:, :], 1.0).then_inc(gT_copied, 1)
                with act.Fori(0, H) as h:
                    with act.Fori(0, NT) as t:
                        n = h * NT + t
                        act.wait_ge(g_shift, n + 1)
                        nc.scalar.activation(g_z, g_z, ACT.Exp, bias=shift[:, :], scale=1.0,
                                             accum_out=rsum[:, :]).then_inc(g_exp, 1)
                        for g in range(NCH):
                            act.wait_ge(g_tr, n * NCH + (g + 1) + 1)
                            act.wait_ge(g_mm, n * NCH + max(g - 1, 0) + 1)
                            scaled(g_p[g % 2], PT[g % 2][:, :], 1.0).then_inc(g_pc, 1)

            if_general(act, general, (gT_copied, g_pc))

        @block.vector
        def _(dve):
            Y = [S[0], S[1], S[2], VF]
            X = [PT[0], PT[1], O, T]

            def lo_part(dst, src, scale, hi):
                return dve.scalar_tensor_tensor(out=dst, in0=src, scalar=scale, in1=hi, op0=ALU.mult,
                                                op1=ALU.subtract)

            dve.memset(sel_v[0:64, :], W_UP * XV_UP / B_UP)
            dve.memset(sel_v[64:P, :], 0.0)
            dve.memset(sel_b[0:64, :], 0.0)
            dve.memset(sel_b[64:P, :], W_UP * X1_UP / B_UP).then_inc(sel_set, 1)

            def wait_apart(semaphore, value):
                dve.wait_ge(semaphore, value)
                dve.nop(nofuse=True)

            for o in range(KC):
                dve.wait_ge(w_hi, o + 1)
                lo_part(w16[:, :, 1, o, :], wf[:, :, o, :], W_UP, w16[:, :, 0, o, :]).then_inc(w_lo, 1)
            dve.wait_ge(bq_hi, 1)
            lo_part(bq16[:, :, 1], bqc[:, :], B_UP, bq16[:, :, 0]).then_inc(bq_lo, 1)
            for ic in range(KC):
                dve.wait_ge(m_hi, ic + 1)
                lo_part(m16[:, 1, ic, :], Y[ic][:, :], 1.0 / W_UP, m16[:, 0, ic, :]).then_inc(m_lo, 1)
            dve.wait_ge(c_ready, 1)
            dve.tensor_reduce(csum[:, :], T[:, 0:2 * KC].rearrange("p (c b) -> p c b", b=2), AX.X, ALU.add
                              ).then_inc(csum_set, 1)
            dve.wait_ge(csum_set, 1)
            dve.tensor_scalar(c8[:, :], csum[:, :], Y_UP * HALF_SCALE / (W_UP * B_UP), None, ALU.mult
                              ).then_inc(c_set, 1)

            def between(n):
                if n == 0:
                    for ic in range(KC):
                        dve.wait_ge(wvT_hi, ic + 1)
                        lo_part(wvT[:, 1, ic, :], X[ic][:, :], W_UP, wvT[:, 0, ic, :]).then_inc(wvT_lo, 1)
                if n == 1:
                    dve.wait_ge(small_in, 16 * 4)
                    dve.tensor_scalar(brh, brf, B_UP, None, ALU.mult).then_inc(br_hi, 1)
                    dve.wait_ge(br_hi, 1)
                    lo_part(brl, brf, B_UP, brh).then_inc(br_lo, 1)
                    dve.wait_ge(br_lo, 1)
                    for k in range(4):
                        last = dve.tensor_copy(brow[32 * k:32 * k + 32, :], (brl if k % 2 else brh)[32 * k:32 * k + 32, :])
                    last.then_inc(br_set, 1)
                if n == 2:
                    dve.wait_ge(w1_hi, 1)
                    lo_part(w1s[:, 1], w1f, W_UP, w1s[:, 0]).then_inc(w1_lo, 1)
                if n in (2, 3):
                    k = n - 2
                    dve.wait_ge(prod_set, (k + 1) * KC)
                    dve.tensor_reduce(u[:, :, k * H:(k + 1) * H], prod[k].rearrange("p c (h d) -> p c h d", h=H),
                                      AX.X, ALU.add).then_inc(u_set, 1)
                if n == 3:
                    dve.wait_ge(u_set, 2)
                    uf = u[:, :, :].rearrange("p c h -> p (c h)")
                    dve.tensor_tensor_reduce(out=usq, in0=uf, in1=uf, scale=1.0, scalar=0.0, op0=ALU.mult,
                                             op1=ALU.add, accum_out=usum[:, :]).then_inc(usq_set, 1)
                if n == 4:
                    dve.wait_ge(const_set, 1)
                    dve.wait_ge(usq_set, 1)
                    for q in range(2):
                        scan(0, 0, q)
                if n == 5:
                    for q in range(2, NQ):
                        scan(0, 0, q)
                    scan_row(0)

            def transposed(g, c):
                for kc in range(KC):
                    dve.wait_ge(xt_hi, g * KC + (kc + 1))
                    cols = bass.ds(g * CH, CH)
                    lo_part(xT[:, 1, kc, cols], X[kc][:, :], XT_UP, xT[:, 0, kc, cols]).then_inc(xt_lo, 1)
                dve.wait_ge(xv_hi, g + 1)
                tiles = bass.ds(g * JB, JB)
                lo_part(xv[:, 1, tiles, :].rearrange("p t n -> p (t n)"), xs[c % 2].rearrange("p t n -> p (t n)"),
                        XV_UP, xv[:, 0, tiles, :].rearrange("p t n -> p (t n)")).then_inc(xv_lo, 1)

            def queries(g, c, jcs):
                for jc in jcs:
                    dve.wait_ge(y_hi, g * KC + (jc + 1))
                    src = yf[jc % 2][:, :].rearrange("p (j n) -> p j n", j=JB)
                    dve.tensor_tensor(ybuf[:, :, 1, jc, :], src, ybuf[:, :, 0, jc, :], ALU.subtract).then_inc(y_lo, 1)

            def scan(t, c, q):
                if q == 0:
                    wait_apart(adj_in, t * 16 + 16)
                part = ring[:, c % SLOTS, q * QW:(q + 1) * QW]
                dve.max(cand[:, q, :], part).then_inc(cand_set, 1)
                wait_apart(cand_set, t * NQ + (q + 1))
                dve.max_index(cidx[:, q, :], cand[:, q, :], part).then_inc(cidx_set, 1)

            def scan_row(t):
                cf = cand[:, :, :].rearrange("p q k -> p (q k)")
                gf = gidx[:, :, :].rearrange("p q k -> p (q k)")
                wait_apart(cand_set, t * NQ + NQ)
                dve.max(top8[:, :], cf).then_inc(top_set, 1)
                dve.wait_ge(cidx_set, t * NQ + NQ)
                dve.tensor_tensor(gf, cidx[:, :, :].rearrange("p q k -> p (q k)"),
                                  offs[:, :, :].rearrange("p q k -> p (q k)"), ALU.add).then_inc(gidx_set, 1)
                dve.wait_ge(top_set, t + 1)
                dve.wait_ge(gidx_set, t + 1)
                dve.scalar_tensor_tensor(out=gf, in0=cf, scalar=top8[:, 0:1], in1=gf, op0=ALU.is_equal,
                                         op1=ALU.mult, accum_out=pickf[:, :]).then_inc(pickf_set, 1)
                dve.tensor_copy(top2[:, bass.ds(t, 1), :].rearrange("p t k -> p (t k)"), top8[:, 0:2]
                                ).then_inc(scan_set, 1)
                dve.wait_ge(pickf_set, t + 1)
                dve.tensor_scalar(pick[:, bass.ds(t, 1)], pickf[:, :], float(N - 1), None, ALU.min
                                  ).then_inc(scan_set, 1)

            def transpose_quarter(t, c, q, halves=(0, 1)):
                if 0 in halves:
                    if c * NQ + q >= 2:
                        dve.wait_ge(pt_lo[q % 2], t * (NQ // 2) + q // 2)
                    wait_apart(p_ready, t * NQ + (q + 1))
                src = ring[:, c % SLOTS, q * QW:(q + 1) * QW].rearrange("p (m b i) -> p m b i", b=4, i=32)
                dst = ET[q % 2][:, :].rearrange("p (m b i) -> p m b i", b=4, i=32)
                for half in halves:
                    for a in (2 * half, 2 * half + 1):
                        for b in range(4):
                            last = dve.transpose(dst[32 * b:32 * b + 32, :, a, :], src[32 * a:32 * a + 32, :, b, :])
                if 1 in halves:
                    last.then_inc(pt_ready, 1)

            def exponentials_lo(t, c, q):
                dve.wait_ge(pt_hi, t * NQ + (q + 1))
                dve.tensor_tensor(pT[:, c % SLOTS, q, 1, :], pt_banks[:, :], pT[:, c % SLOTS, q, 0, :], ALU.subtract
                                  ).then_inc(pt_lo[1], 1)

            def beside(s, c, k):
                if c == 0 and 3 <= k < 3 + NQ:
                    scan(1, 1, k - 3)
                if c == 0 and k == 3 + NQ:
                    scan_row(1)
                if c == 1 and k < 6:
                    transpose_quarter(0, 0, 1 + k // 2, (k % 2,))
                if c == 1 and k == 3:
                    exponentials_lo(0, 0, 1)
                if c == 1 and k == 7:
                    exponentials_lo(0, 0, 3)
                if c >= 2 and k in (2, 3):
                    transpose_quarter(s - 1, c - 1, NQ - 1, (k - 2,))
                if c >= 2 and k == 4:
                    exponentials_lo(s - 1, c - 1, NQ - 1)
                if 2 <= c < NT - 1 and k in (4, 6):
                    scan(s + 1, c + 1, (k - 4) // 2)

            def logits(s, c, k):
                if k == 0:
                    dve.wait_ge(cidx_set, s * NQ + NQ)
                wait_apart(s_ready, s * NCH + (k + 1))
                part = ring[:, c % SLOTS, k * CH:(k + 1) * CH]
                dve.tensor_tensor_reduce(out=part, in0=S[(c * NCH + k) % 3][:, :], in1=part, scale=1.0,
                                         scalar=-3.0e38, op0=ALU.add, op1=ALU.max,
                                         accum_out=cmax[:, k:k + 1]).then_inc(s_used, 1)
                beside(s, c, k)

            def step(s, c):
                score, value, follow = c < NT, 1 <= c <= NT, c >= 2
                if c == NT:
                    transpose_quarter(s - 1, c - 1, NQ - 1)
                    exponentials_lo(s - 1, c - 1, NQ - 1)
                if score:
                    logits(s, c, 0)
                if value:
                    dve.wait_ge(p_ready, s * NQ)
                    dve.tensor_reduce(rsum[:, :], sums[:, :], AX.X, ALU.add).then_inc(rsum_set, 1)
                if score:
                    logits(s, c, 1)
                if value:
                    dve.wait_ge(rsum_set, s)
                    if c >= 2:
                        dve.wait_ge(ctx_set, s - 1)
                    dve.reciprocal(rinv[:, :], rsum[:, :]).then_inc(rinv_set, 1)
                if follow:
                    dve.wait_ge(ctxT_hi, s - 1)
                    lo_part(postT[:, 1].rearrange("p c n -> p (c n)"), T[:, :], 1.0,
                            postT[:, 0].rearrange("p c n -> p (c n)")).then_inc(ctxT_lo, 1)
                if score:
                    logits(s, c, 2)
                    logits(s, c, 3)
                if follow:
                    dve.wait_ge(v_ready, s - 1)
                    dve.wait_ge(res_in, s * 16 - 16)
                    dve.scalar_tensor_tensor(out=res[:, :], in0=VF[:, :], scalar=1.0 / (W_UP * XV_UP), in1=res[:, :],
                                             op0=ALU.mult, op1=ALU.add).then_inc(h_set, 1)
                    dve.wait_ge(h_set, s - 1)
                    dve.bn_stats(stats[:, :], res[:, :]).then_inc(stats_set, 1)
                    wait_apart(stats_set, s - 1)
                    dve.bn_aggr(mv[:, :], stats[:, :]).then_inc(mv_set, 1)
                if score:
                    logits(s, c, 4)
                if follow:
                    dve.wait_ge(rstd_set, s - 1)
                    dve.tensor_scalar(res[:, :], res[:, :], mv[:, 0:1], rstd[:, :], ALU.subtract, ALU.mult
                                      ).then_inc(x1_set, 1)
                if score:
                    logits(s, c, 5)
                if score:
                    logits(s, c, 6)
                if follow:
                    dve.wait_ge(x1T_hi, s - 1)
                    lo_part(postT[:, 1].rearrange("p c n -> p (c n)"), T[:, :], X1_UP,
                            postT[:, 0].rearrange("p c n -> p (c n)")).then_inc(x1T_lo, 1)
                if score:
                    logits(s, c, 7)
                    dve.wait_ge(s_used, (s + 1) * NCH)
                    dve.tensor_reduce(rmax[:, :], cmax[:, :], AX.X, ALU.max).then_inc(rmax_set, 1)
                    dve.wait_ge(rmax_set, s + 1)
                    if c >= 1:
                        dve.wait_ge(p_ready, s * NQ)
                    dve.tensor_scalar(shift[:, :], rmax[:, :], -2.0, P_LOG2 * LN2, ALU.mult, ALU.add
                                      ).then_inc(shift_set, 1)
                for q in range(NQ):
                    if c == 0 and q == 0:
                        transpose_quarter(0, 0, 0)
                    if score and c >= 1 and q < NQ - 1:
                        transpose_quarter(s, c, q)
                    if score and c >= 1 and q == 2:
                        exponentials_lo(s, c, 1)
                    if c == 1 or 2 <= c < NT - 1 and q < 2:
                        scan(s + 1, c + 1, q if c == 1 else q + 2)
                    if c == 1 and q == NQ - 1 or 2 <= c < NT - 1 and q == 2:
                        scan_row(s + 1)

            def prove_single():
                t2 = top2[:, :, :].rearrange("p t k -> p (t k)")
                mask, mag = okw[:, 64:128], okw[:, 128:192]
                by_row = mask.rearrange("p (t k) -> p t k", k=2)
                need, gap = okw[:, 192:224], okw[:, 224:256]
                steps = [0]

                def then(ins):
                    steps[0] += 1
                    ins.then_inc(ok_chain, 1)
                    dve.wait_ge(ok_chain, steps[0])

                dve.wait_ge(usum_ready, 1)
                dve.tensor_scalar(thr[:, :], S[1][:, 0:1], 64.0, 64.0 + 200.0, ALU.mult, ALU.add).then_inc(thr_set, 1)
                dve.wait_ge(thr_set, 1)
                dve.wait_ge(scan_set, 2 * NT)
                then(dve.tensor_scalar(mask, t2, -1.0, 1.0, ALU.mult, ALU.add))
                then(dve.tensor_scalar(mask, mask, NEG_INF, None, ALU.mult))
                then(dve.scalar_tensor_tensor(out=mag, in0=mask, scalar=-1.0, in1=mask, op0=ALU.mult, op1=ALU.max))
                by_row_mag = mag.rearrange("p (t k) -> p t k", k=2)
                then(dve.tensor_tensor(need, by_row_mag[:, :, 0], by_row_mag[:, :, 1], ALU.add))
                then(dve.tensor_scalar(need, need, 2.0 ** -22, thr[:, :], ALU.mult, ALU.add))
                then(dve.tensor_tensor(gap, by_row[:, :, 0], by_row[:, :, 1], ALU.subtract))
                then(dve.tensor_tensor(gap, gap, need, ALU.is_ge))
                then(dve.tensor_reduce(okw[:, 0:1], gap, AX.X, ALU.add))

            def last_rstd(e):
                of_var, sign = (1.0 / D, 1.0) if e % 2 else (1.0, -1.0)
                t = slice(e * JB, (e + 1) * JB)
                dve.wait_ge(e_sd, e + 1)
                dve.reciprocal(e_r[:, t], e_s[:, t]).then_inc(e_chain, 1)
                dve.wait_ge(e_chain, e * 5 + 1)
                dve.tensor_tensor(e_t[:, t], e_r[:, t], e_r[:, t], ALU.mult).then_inc(e_chain, 1)
                dve.wait_ge(e_chain, e * 5 + 2)
                dve.scalar_tensor_tensor(out=e_t[:, t], in0=e_mean[:, t, 1], scalar=EPS / of_var, in1=e_t[:, t], op0=ALU.add,
                                         op1=ALU.mult).then_inc(e_chain, 1)
                dve.wait_ge(e_chain, e * 5 + 3)
                dve.tensor_scalar(e_t[:, t], e_t[:, t], -0.5 * of_var, 1.5, ALU.mult, ALU.add).then_inc(e_chain, 1)
                dve.wait_ge(e_chain, e * 5 + 4)
                dve.tensor_tensor(e_r[:, t], e_r[:, t], e_t[:, t], ALU.mult).then_inc(e_chain, 1)
                dve.wait_ge(e_chain, e * 5 + 5)
                dve.scalar_tensor_tensor(out=e_nm[:, t], in0=e_mean[:, t, 0], scalar=sign, in1=e_r[:, t],
                                         op0=ALU.mult, op1=ALU.mult).then_inc(e_rstd, 1)

            def last_norm():
                for e in range(NE):
                    tiles = range(e * JB, (e + 1) * JB)
                    dve.wait_ge(x1r_in[e], 32 if e == NE - 1 else 16)
                    dve.wait_ge(got_in[e], 16 * JB)
                    for t in tiles:
                        dve.scalar_tensor_tensor(out=got[:, t, :], in0=got[:, t, :], scalar=0.0, in1=x1r[:, t, :],
                                                 op0=ALU.max, op1=ALU.add,
                                                 accum_out=e_tot[:, t:t + 1]).then_inc(e_sum, 1)
                    if e % 2:
                        dve.wait_ge(e_sum, (e + 1) * JB)
                        dve.tensor_scalar(e_mean[:, tiles[0]:tiles[-1] + 1, 0], e_tot[:, tiles[0]:tiles[-1] + 1],
                                          -1.0 / D, None, ALU.mult).then_inc(e_neg, 1)
                    else:
                        for t in tiles:
                            dve.wait_ge(e_sum, t + 1)
                            dve.bn_stats(e_st[:, t, :], got[:, t, :]).then_inc(e_stats, 1)
                        for n, t in enumerate(tiles):
                            dve.wait_ge(e_stats, e // 2 * JB + n + 1)
                            dve.bn_aggr(e_mean[:, t, :], e_st[:, t, :]).then_inc(e_mv, 1)
                    if e >= 1:
                        last_rstd(e - 1)
                last_rstd(NE - 1)

            run_groups(dve, transposed, queries, between)
            run_steps(dve, step, NT // 3 - 1)
            prove_single()
            last_norm()
            dve.wait_ge(count_ready, 1)
            dve.tensor_copy(flag[:, :], S[0][0:1, 0:1]).then_inc(flag_set, 1)

            def general():
                with dve.Fori(0, NT) as t:
                    dve.wait_ge(ge_ready, t + 2)
                    dve.tensor_copy(g_enT[:, bass.ds(t * P, P)], S[0][0:H, 0:P]).then_inc(ge_copied, 1)
                    dve.tensor_copy(g_es[:, bass.ds(t, 1), :].rearrange("p t h -> p (t h)"), S[1][:, 0:H]
                                    ).then_inc(ge_copied, 1)
                dve.wait_ge(gen_out, 16)
                dve.wait_ge(ge_copied, 2 * NT + 1)
                with dve.Fori(0, H) as h:
                    with dve.Fori(0, NT) as t:
                        n = h * NT + t
                        dve.wait_ge(ga_in, n * 16 + 16)
                        dve.tensor_scalar(g_adj, g_adj, -1.0, 1.0, ALU.mult, ALU.add).then_inc(g_mask, 1)
                        dve.tensor_copy(thr[:, :], g_es[:, bass.ds(t, 1), bass.ds(h, 1)]
                                        .rearrange("p t h -> p (t h)")).then_inc(g_mask, 1)
                        dve.wait_ge(g_mask, n * 3 + 2)
                        dve.tensor_scalar(g_adj, g_adj, NEG_INF, None, ALU.mult).then_inc(g_mask, 1)
                        dve.wait_ge(gnb_in, h * 16 + 16)
                        dve.wait_ge(g_tr, n * NCH + 1)
                        dve.tensor_scalar(g_z, g_nb, thr[:, :], None, ALU.add).then_inc(g_z_set, 1)
                        dve.wait_ge(g_z_set, n + 2)
                        dve.scalar_tensor_tensor(out=g_z, in0=g_z, scalar=0.2, in1=g_z, op0=ALU.mult, op1=ALU.max
                                                 ).then_inc(g_inv, 1)
                        dve.wait_ge(g_inv, n * 3 + 1)
                        wait_apart(g_mask, n * 3 + 3)
                        dve.tensor_tensor_reduce(out=g_z, in0=g_z, in1=g_adj, scale=1.0, scalar=-3.0e38, op0=ALU.add,
                                                 op1=ALU.max, accum_out=rmax[:, :]).then_inc(g_log, 1)
                        dve.wait_ge(g_log, n + 2)
                        dve.tensor_scalar(shift[:, :], rmax[:, :], -1.0, None, ALU.mult).then_inc(g_shift, 1)
                        dve.wait_ge(g_exp, n + 1)
                        dve.reciprocal(rinv[:, :], rsum[:, :]).then_inc(g_inv, 1)
                        dve.wait_ge(g_inv, n * 3 + 2)
                        dve.wait_ge(g_mm, n * NCH + NCH + 1)
                        dve.tensor_scalar(g_row, O[:, 0:DH], rinv[:, :], None, ALU.mult).then_inc(g_inv, 1)
                        dve.wait_ge(g_inv, n * 3 + 3)
                        dve.tensor_copy(g_out[:, bass.ds(t, 1), bass.ds(h * DH, DH)].rearrange("p t d -> p (t d)"),
                                        g_row).then_inc(g_o, 1)
                dve.wait_ge(g_o, H * NT + 1)
                with dve.Fori(0, NT) as t:
                    dve.wait_ge(gx_in, t * 16 + 16 * (NT + 1))
                    dve.scalar_tensor_tensor(out=res[:, :], in0=g_out[:, bass.ds(t, 1), :].rearrange("p t d -> p (t d)"),
                                             scalar=0.0, in1=res[:, :], op0=ALU.max, op1=ALU.add).then_inc(gh_set, 1)
                    dve.wait_ge(gh_set, t + 1)
                    dve.bn_stats(stats[:, :], res[:, :]).then_inc(gh_stats, 1)
                    wait_apart(gh_stats, t + 1)
                    dve.bn_aggr(mv[:, :], stats[:, :]).then_inc(gh_mv, 1)
                    dve.wait_ge(gh_rstd, t + 1)
                    dve.tensor_scalar(res[:, :], res[:, :], mv[:, 0:1], rstd[:, :], ALU.subtract, ALU.mult
                                      ).then_inc(gh_fin, 1)

            if_general(dve, general, (ge_copied, g_z_set, g_log, g_o))


_INS = ["x", "adj", "L0_gnn_Wq", "L0_gnn_bq", "L0_gnn_Wk", "L0_gnn_Wv", "L0_gnn_bv", "L1_gnn_W", "L1_gnn_b",
        "L1_gnn_a_self", "L1_gnn_a_neigh"]


def kernel(**inputs):
    import numpy as np
    import concourse.bacc as bacc
    from concourse.bass_utils import run_bass_kernel_spmd

    nc = bacc.Bacc("TRN2", target_bir_lowering=False, num_devices=1)
    arrays, args = {}, []
    for name in _INS:
        a = np.ascontiguousarray(inputs[name])
        arrays[f"in_{name}"] = a
        args.append(nc.dram_tensor(f"in_{name}", a.shape, mybir.dt.from_np(a.dtype), kind="ExternalInput").ap())
    out = nc.dram_tensor("out", inputs["x"].shape, F32, kind="ExternalOutput").ap()
    adj_resnorm_kernel(nc, *args, out)
    r = run_bass_kernel_spmd(nc, [arrays], core_ids=[0])
    return r.results[0]["out"]
```
